# Optimizing a Trainium2 kernel written in Bass

```python
import numpy as np
import jax
import jax.numpy as jnp

def _softmax(x, axis=-1):
    return jax.nn.softmax(x, axis=axis)

def _gelu(x):
    return jax.nn.gelu(x, approximate=True)

def _silu(x):
    return jax.nn.silu(x)

def _sigmoid(x):
    return jax.nn.sigmoid(x)

def _layernorm(x, axis=-1, eps=1e-05):
    m = jnp.mean(x, axis=axis, keepdims=True)
    v = jnp.var(x, axis=axis, keepdims=True)
    return (x - m) / jnp.sqrt(v + eps)

def _scatter_add(tgt, idx, src, axis=0):
    return tgt.at[idx].add(src)

def _segment_sum(src, seg, n):
    return jax.ops.segment_sum(src, seg, n)
kernel_name = 'mk_gnn_resnorm_d4_gnn_r8_8b0f88'

def setup_inputs(seed: int=0):
    np.random.seed(seed)
    _w = jnp.asarray

    def _rec_inputs():
        import jax
        import jax.numpy as jnp
        _gk = jax.random.key(seed)
        x = -0.0005121 + 1.001 * jax.random.normal(jax.random.fold_in(_gk, 1), (12500, 32), jnp.float32)
        _s = jax.random.randint(jax.random.fold_in(_gk, 2), (100000,), 0, 12500, jnp.int32)
        _d = jax.random.randint(jax.random.fold_in(_gk, 3), (100000,), 0, 12500, jnp.int32)
        _loop = jnp.arange(12500, dtype=jnp.int32)
        src = jnp.concatenate([_s, _d, _loop])
        dst = jnp.concatenate([_d, _s, _loop])
        _o = jnp.argsort(dst, stable=True)
        src = src[_o]
        dst = dst[_o]
        edge_attr_3 = jax.random.uniform(jax.random.fold_in(_gk, 11), (212500, 3), jnp.float32, 0.0, 1)
        return (x, src, dst, edge_attr_3)
    x, src, dst, edge_attr_3 = _rec_inputs()

    def _L0_gnn_setup():
        import jax, jax.numpy as jnp
        import numpy as np
        N = 12500
        E = 200000
        IN_C, HID_C, OUT_C = (32, 64, 32)

        def _gin_conv(x, src, dst, W_a, b_a, W_b, b_b):
            agg = jax.ops.segment_sum(x[src], dst, num_segments=N)
            h = agg + x
            h = jax.nn.relu(h @ W_a + b_a)
            return h @ W_b + b_b
        key = jax.random.key(seed)
        ks = jax.random.split(key, 10)
        x = jax.random.normal(ks[0], (N, IN_C), dtype=jnp.float32)
        edge_index = jax.random.randint(ks[1], (2, E), 0, N, dtype=jnp.int64)

        def lin(k, fan_in, fan_out):
            kw, kb = jax.random.split(k)
            bound = 1.0 / np.sqrt(fan_in)
            W = jax.random.uniform(kw, (fan_in, fan_out), minval=-bound, maxval=bound, dtype=jnp.float32)
            b = jax.random.uniform(kb, (fan_out,), minval=-bound, maxval=bound, dtype=jnp.float32)
            return (W, b)
        W1, b1 = lin(ks[2], IN_C, HID_C)
        W2, b2 = lin(ks[3], HID_C, HID_C)
        W3, b3 = lin(ks[4], HID_C, HID_C)
        W4, b4 = lin(ks[5], HID_C, OUT_C)
        return {'x': x, 'edge_index': edge_index, 'W1': W1, 'b1': b1, 'W2': W2, 'b2': b2, 'W3': W3, 'b3': b3, 'W4': W4, 'b4': b4}
    _L0_gnn_all = _L0_gnn_setup()
    _L0_gnn_in = {k: v for k, v in _L0_gnn_all.items() if k in ('W1', 'b1', 'W2', 'b2', 'W3', 'b3', 'W4', 'b4')}
    del _L0_gnn_all

    def _L1_gnn_setup():
        import jax, jax.numpy as jnp
        import numpy as np
        K = 2
        N_NODES = 12500
        N_EDGES = 200000
        D_FEAT = 32
        key = jax.random.key(seed)
        k1, k2 = jax.random.split(key)
        x = jax.random.normal(k1, (N_NODES, D_FEAT), dtype=jnp.float32)
        edge_index = jax.random.randint(k2, (2, N_EDGES), 0, N_NODES, dtype=jnp.int32)
        return {'x': x, 'edge_index': edge_index}
    _L1_gnn_all = _L1_gnn_setup()
    _L1_gnn_in = {k: v for k, v in _L1_gnn_all.items() if k in ()}
    del _L1_gnn_all

    def _L2_gnn_setup():
        import jax, jax.numpy as jnp
        import numpy as np
        N = 6250
        E = 200000
        C = 32
        KS = 4
        DIM = 3
        K3 = KS ** DIM
        NEG = 0.01
        EPS = 1e-05
        _BITS = np.array([[s >> d & 1 for d in range(DIM)] for s in range(2 ** DIM)], dtype=np.int32)

        def _basis(edge_attr):
            v = edge_attr * (KS - 1)
            lo = jnp.floor(v)
            f = v - lo
            lo = lo.astype(jnp.int32)
            bits = jnp.asarray(_BITS)
            idx = jnp.clip(lo[:, None, :] + bits[None], 0, KS - 1)
            w = jnp.where(bits[None] == 1, f[:, None, :], 1.0 - f[:, None, :])
            basis = jnp.prod(w, axis=-1)
            wi = idx[..., 0] + KS * idx[..., 1] + KS * KS * idx[..., 2]
            return (basis, wi)

        def _sconv(x, src, dst, basis, wi, W, R, b):
            n = x.shape[0]
            z = jnp.einsum('nc,kco->nko', x, W)
            msg = jnp.zeros((src.shape[0], W.shape[2]), x.dtype)
            for s in range(basis.shape[1]):
                msg = msg + basis[:, s, None] * z[src, wi[:, s]]
            agg = jax.ops.segment_sum(msg, dst, num_segments=n)
            cnt = jax.ops.segment_sum(jnp.ones((dst.shape[0],), x.dtype), dst, num_segments=n)
            agg = agg / jnp.clip(cnt, 1.0)[:, None]
            return agg + x @ R + b

        def _bn(x, g, be):
            mu = x.mean(0)
            var = x.var(0)
            return (x - mu) * jax.lax.rsqrt(var + EPS) * g + be

        def _leaky(x):
            return jnp.where(x >= 0, x, NEG * x)
        key = jax.random.key(seed)
        ks = jax.random.split(key, 32)
        inp = {'patch_embs': jax.random.normal(ks[0], (N, C), jnp.float32), 'edge_index': jax.random.randint(ks[1], (2, E), 0, N, jnp.int32), 'edge_attr': jax.random.uniform(ks[2], (E, DIM), jnp.float32)}
        i = 3
        for l in (1, 2, 3):
            inp[f'W{l}'] = jax.random.normal(ks[i], (K3, C, C), jnp.float32) * 0.05
            i += 1
            inp[f'R{l}'] = jax.random.normal(ks[i], (C, C), jnp.float32) * 0.1
            i += 1
            inp[f'b{l}'] = jnp.zeros((C,), jnp.float32)
            inp[f'g{l}'] = jnp.ones((C,), jnp.float32)
            inp[f'be{l}'] = jnp.zeros((C,), jnp.float32)
        return inp
    _L2_gnn_all = _L2_gnn_setup()
    _L2_gnn_in = {k: v for k, v in _L2_gnn_all.items() if k in ('W1', 'R1', 'b1', 'g1', 'be1', 'W2', 'R2', 'b2', 'g2', 'be2', 'W3', 'R3', 'b3', 'g3', 'be3')}
    del _L2_gnn_all

    def _L3_gnn_setup():
        import jax, jax.numpy as jnp
        import numpy as np
        N_NODES = 6250
        DEG = 16
        N_HEAD = 4
        F_IN = 32
        F_OUT = 32
        key = jax.random.key(seed)
        k_h, k_w, k_fw, k_fb = jax.random.split(key, 4)
        h = jax.random.normal(k_h, (N_NODES, F_IN), dtype=jnp.float32)
        src = jnp.repeat(jnp.arange(N_NODES, dtype=jnp.int64), DEG)
        offs = (jnp.arange(DEG, dtype=jnp.int64) + 1) * 97
        dst = (src.reshape(N_NODES, DEG) + offs[None, :]).reshape(-1) % N_NODES
        edge_index = jnp.stack([src, dst], axis=0)
        gain = 1.414
        bound_w = gain * np.sqrt(6.0 / (F_IN + F_OUT))
        w = jax.random.uniform(k_w, (N_HEAD, F_IN, F_OUT), jnp.float32, -bound_w, bound_w)
        bound_fc = np.sqrt(1.0 / (2 * F_OUT))
        fc_w = jax.random.uniform(k_fw, (1, 2 * F_OUT), jnp.float32, -bound_fc, bound_fc)
        fc_b = jax.random.uniform(k_fb, (1,), jnp.float32, -bound_fc, bound_fc)
        bias = jnp.zeros((F_OUT,), jnp.float32)
        return {'h': h, 'edge_index': edge_index, 'w': w, 'fc_w': fc_w, 'fc_b': fc_b, 'bias': bias}
    _L3_gnn_all = _L3_gnn_setup()
    _L3_gnn_in = {k: v for k, v in _L3_gnn_all.items() if k in ('w', 'fc_w', 'fc_b', 'bias')}
    del _L3_gnn_all
    return {'x': x, 'src': src, 'dst': dst, 'edge_attr_3': edge_attr_3, 'L0_gnn_W1': _L0_gnn_in['W1'], 'L0_gnn_b1': _L0_gnn_in['b1'], 'L0_gnn_W2': _L0_gnn_in['W2'], 'L0_gnn_b2': _L0_gnn_in['b2'], 'L0_gnn_W3': _L0_gnn_in['W3'], 'L0_gnn_b3': _L0_gnn_in['b3'], 'L0_gnn_W4': _L0_gnn_in['W4'], 'L0_gnn_b4': _L0_gnn_in['b4'], 'L2_gnn_W1': _L2_gnn_in['W1'], 'L2_gnn_R1': _L2_gnn_in['R1'], 'L2_gnn_b1': _L2_gnn_in['b1'], 'L2_gnn_g1': _L2_gnn_in['g1'], 'L2_gnn_be1': _L2_gnn_in['be1'], 'L2_gnn_W2': _L2_gnn_in['W2'], 'L2_gnn_R2': _L2_gnn_in['R2'], 'L2_gnn_b2': _L2_gnn_in['b2'], 'L2_gnn_g2': _L2_gnn_in['g2'], 'L2_gnn_be2': _L2_gnn_in['be2'], 'L2_gnn_W3': _L2_gnn_in['W3'], 'L2_gnn_R3': _L2_gnn_in['R3'], 'L2_gnn_b3': _L2_gnn_in['b3'], 'L2_gnn_g3': _L2_gnn_in['g3'], 'L2_gnn_be3': _L2_gnn_in['be3'], 'L3_gnn_w': _L3_gnn_in['w'], 'L3_gnn_fc_w': _L3_gnn_in['fc_w'], 'L3_gnn_fc_b': _L3_gnn_in['fc_b'], 'L3_gnn_bias': _L3_gnn_in['bias']}

def reference(x, src, dst, edge_attr_3, L0_gnn_W1, L0_gnn_b1, L0_gnn_W2, L0_gnn_b2, L0_gnn_W3, L0_gnn_b3, L0_gnn_W4, L0_gnn_b4, L2_gnn_W1, L2_gnn_R1, L2_gnn_b1, L2_gnn_g1, L2_gnn_be1, L2_gnn_W2, L2_gnn_R2, L2_gnn_b2, L2_gnn_g2, L2_gnn_be2, L2_gnn_W3, L2_gnn_R3, L2_gnn_b3, L2_gnn_g3, L2_gnn_be3, L3_gnn_w, L3_gnn_fc_w, L3_gnn_fc_b, L3_gnn_bias):
    import jax
    import jax.numpy as jnp

    def _L0_gnn_ref(x, edge_index, W1, b1, W2, b2, W3, b3, W4, b4):
        import jax, jax.numpy as jnp
        import numpy as np
        N = 12500
        E = 200000
        IN_C, HID_C, OUT_C = (32, 64, 32)

        def _gin_conv(x, src, dst, W_a, b_a, W_b, b_b):
            agg = jax.ops.segment_sum(x[src], dst, num_segments=N)
            h = agg + x
            h = jax.nn.relu(h @ W_a + b_a)
            return h @ W_b + b_b
        src, dst = (edge_index[0], edge_index[1])
        h = jax.nn.relu(_gin_conv(x, src, dst, W1, b1, W2, b2))
        out = _gin_conv(h, src, dst, W3, b3, W4, b4)
        return out

    def _L1_gnn_ref(x, edge_index):
        import jax, jax.numpy as jnp
        import numpy as np
        K = 2
        N_NODES = 12500
        N_EDGES = 200000
        D_FEAT = 32
        n = x.shape[0]
        x = jax.nn.relu(x)
        loops = jnp.arange(n, dtype=edge_index.dtype)
        src = jnp.concatenate([edge_index[0], loops])
        dst = jnp.concatenate([edge_index[1], loops])
        deg = jax.ops.segment_sum(jnp.ones_like(src, dtype=x.dtype), dst, num_segments=n)
        dinv = jax.lax.rsqrt(jnp.maximum(deg, 1.0))
        norm = (dinv[src] * dinv[dst])[:, None]
        for _ in range(K):
            x = jax.ops.segment_sum(x[src] * norm, dst, num_segments=n)
        return x

    def _L2_gnn_ref(patch_embs, edge_index, edge_attr, W1, R1, b1, g1, be1, W2, R2, b2, g2, be2, W3, R3, b3, g3, be3):
        import jax, jax.numpy as jnp
        import numpy as np
        N = 6250
        E = 200000
        C = 32
        KS = 4
        DIM = 3
        K3 = KS ** DIM
        NEG = 0.01
        EPS = 1e-05
        _BITS = np.array([[s >> d & 1 for d in range(DIM)] for s in range(2 ** DIM)], dtype=np.int32)

        def _basis(edge_attr):
            v = edge_attr * (KS - 1)
            lo = jnp.floor(v)
            f = v - lo
            lo = lo.astype(jnp.int32)
            bits = jnp.asarray(_BITS)
            idx = jnp.clip(lo[:, None, :] + bits[None], 0, KS - 1)
            w = jnp.where(bits[None] == 1, f[:, None, :], 1.0 - f[:, None, :])
            basis = jnp.prod(w, axis=-1)
            wi = idx[..., 0] + KS * idx[..., 1] + KS * KS * idx[..., 2]
            return (basis, wi)

        def _sconv(x, src, dst, basis, wi, W, R, b):
            n = x.shape[0]
            z = jnp.einsum('nc,kco->nko', x, W)
            msg = jnp.zeros((src.shape[0], W.shape[2]), x.dtype)
            for s in range(basis.shape[1]):
                msg = msg + basis[:, s, None] * z[src, wi[:, s]]
            agg = jax.ops.segment_sum(msg, dst, num_segments=n)
            cnt = jax.ops.segment_sum(jnp.ones((dst.shape[0],), x.dtype), dst, num_segments=n)
            agg = agg / jnp.clip(cnt, 1.0)[:, None]
            return agg + x @ R + b

        def _bn(x, g, be):
            mu = x.mean(0)
            var = x.var(0)
            return (x - mu) * jax.lax.rsqrt(var + EPS) * g + be

        def _leaky(x):
            return jnp.where(x >= 0, x, NEG * x)
        src, dst = (edge_index[0], edge_index[1])
        basis, wi = _basis(edge_attr)
        x = _bn(_leaky(_sconv(patch_embs, src, dst, basis, wi, W1, R1, b1)) + patch_embs, g1, be1)
        x = _bn(_leaky(_sconv(x, src, dst, basis, wi, W2, R2, b2)) + x, g2, be2)
        x = _bn(_sconv(x, src, dst, basis, wi, W3, R3, b3) + x, g3, be3)
        return x

    def _L3_gnn_ref(h, edge_index, w, fc_w, fc_b, bias):
        import jax, jax.numpy as jnp
        import numpy as np
        N_NODES = 6250
        DEG = 16
        N_HEAD = 4
        F_IN = 32
        F_OUT = 32
        n_head, f_in, f_out = w.shape
        n = h.shape[0]
        src, dst = (edge_index[0], edge_index[1])
        hp = jnp.einsum('nf,hfo->hno', h, w)
        w_src = fc_w[0, :f_out]
        w_dst = fc_w[0, f_out:]
        a_src = jnp.einsum('hnf,f->hn', hp, w_src)
        a_dst = jnp.einsum('hnf,f->hn', hp, w_dst)
        e = a_src[:, src] + a_dst[:, dst] + fc_b[0]
        e = jax.nn.leaky_relu(e, negative_slope=0.2)
        seg_max = jax.ops.segment_max(e.T, src, num_segments=n)
        e = jnp.exp(e - seg_max.T[:, src])
        seg_sum = jax.ops.segment_sum(e.T, src, num_segments=n)
        att = e / seg_sum.T[:, src]
        msg = att[:, :, None] * hp[:, dst, :]
        agg = jax.vmap(lambda m: jax.ops.segment_sum(m, src, num_segments=n))(msg)
        out = agg.mean(axis=0) + bias
        return out
    edge_index = jnp.stack([src, dst])
    x = _layernorm(x + _L0_gnn_ref(x, edge_index, L0_gnn_W1, L0_gnn_b1, L0_gnn_W2, L0_gnn_b2, L0_gnn_W3, L0_gnn_b3, L0_gnn_W4, L0_gnn_b4), axis=-1)
    x = _layernorm(x + _L1_gnn_ref(x, edge_index), axis=-1)
    x = _layernorm(x + _L2_gnn_ref(x, edge_index, edge_attr_3, L2_gnn_W1, L2_gnn_R1, L2_gnn_b1, L2_gnn_g1, L2_gnn_be1, L2_gnn_W2, L2_gnn_R2, L2_gnn_b2, L2_gnn_g2, L2_gnn_be2, L2_gnn_W3, L2_gnn_R3, L2_gnn_b3, L2_gnn_g3, L2_gnn_be3), axis=-1)
    x = _layernorm(x + _L3_gnn_ref(x, edge_index, L3_gnn_w, L3_gnn_fc_w, L3_gnn_fc_b, L3_gnn_bias), axis=-1)
    return x

_drawn_inputs = setup_inputs


def setup_inputs(seed=0):
    import zlib

    import numpy as np

    out = dict(_drawn_inputs(seed))
    spreads = {'L2_gnn_b1': (0.0, 0.1),
     'L2_gnn_g1': (1.0, 0.2),
     'L2_gnn_be1': (0.0, 0.79),
     'L2_gnn_b2': (0.0, 0.299),
     'L2_gnn_g2': (1.0, 0.2),
     'L2_gnn_be2': (0.0, 0.8),
     'L2_gnn_b3': (0.0, 0.8),
     'L2_gnn_g3': (1.0, 0.2),
     'L2_gnn_be3': (0.0, 0.1),
     'L3_gnn_bias': (0.0, 0.1)}
    factors = {'L0_gnn_b3': 4.44, 'L2_gnn_W2': 3.702, 'L2_gnn_W3': 2.914}
    for name, (base, spread) in spreads.items():
        noise = np.random.default_rng([zlib.crc32(name.encode()), seed]).standard_normal(out[name].shape)
        drawn = base * np.exp(spread * noise) if base else spread * noise
        out[name] = jnp.asarray(drawn.astype(out[name].dtype))
    for name, factor in factors.items():
        out[name] = (out[name] * factor).astype(out[name].dtype)
    return out
```

```python
from contextlib import ExitStack

import concourse.bass as bass
from concourse import mybir

F32 = mybir.dt.float32
I32 = mybir.dt.int32
ALU = mybir.AluOpType
ACT = mybir.ActivationFunctionType
AX = mybir.AxisListType

P = 128
N = 12500
C = 32
HID = 64
NT = -(-N // P)
NP = NT * P
LAST_ROWS = N - (NT - 1) * P
E = 212500
G = 16
SUB = 4
SUBS = G // SUB
ET = 1664
TURNS = ET // (2 * G)
WIN = P
BT = 7
BN = BT * P
BLOCKS = NT // BT
RCH = ET // P
KS = 4
K12 = KS * KS
BASIS = KS + K12
HEADS = 4
SCAL = 2 * HEADS
L3ROW = C + SCAL
BIG = 1.0e30
EPS = 1e-5
assert ET * P >= E and NT % BT == 0 and BLOCKS % 2 == 0 and ET % P == 0


class Signal:

    def __init__(self, sem, plan, lead=0):
        self.sem, self.lead, self.base, n = sem, lead, {}, 0
        for phase, events in plan.items():
            self.base[phase] = n
            n += events

    def done(self, phase, k):
        return k + (self.base[phase] + self.lead + 1)


def build(nc, x, src_tile, dst_tile, dst_base, src_row, dst_ext, attr_tile, gW1, gb1, gW2, gb2, gW3, gb3,
          gW4, gb4, sW, sR, sb_, sg, sbe, aw, fc_w, fc_b, abias, out):
    ctx = ExitStack()
    with ctx:
        def sb(name, shape, dt=F32):
            return ctx.enter_context(nc.sbuf_tensor(name, shape, dt))

        def sem(name):
            return ctx.enter_context(nc.semaphore(name))

        tab_h = nc.dram_tensor("tab_h", [NP, HID], F32).ap()
        tabs = {n: nc.dram_tensor(f"tab_{n}", [NP, C], F32).ap() for n in ("gcn1", "gcn2", "sp1", "sp2", "sp3")}
        tab_att = nc.dram_tensor("tab_att", [NP, L3ROW], F32).ap()
        basis_d = nc.dram_tensor("basis_d", [P, ET * BASIS], F32).ap()
        edge_rows = nc.dram_tensor("edge_rows", [P, ET * L3ROW], F32).ap()
        TABLE = {"gin1": x, "gin2": tab_h, "gcn1": tabs["gcn1"], "gcn2": tabs["gcn2"], "sp1": tabs["sp1"],
                 "sp2": tabs["sp2"], "sp3": tabs["sp3"], "collect": tab_att}
        ROW = {p: C for p in TABLE}
        ROW["gin2"], ROW["collect"] = HID, L3ROW
        PASSES = ["gin1", "gin2", "gcn1", "gcn2", "sp1", "sp2", "sp3", "collect", "apply"]
        SPLINE = ["sp1", "sp2", "sp3"]

        big = sb("big", [P, SCAL * ET])
        acc = big[:, 0:NP + WIN]
        rowch = big[:, :].rearrange("p (c e) -> p c e", c=SCAL)
        nodes = sb("nodes", [P, SCAL * ET])
        yn = nodes[:, 0:NT * C].rearrange("p (t c) -> p t c", c=C)
        rn = nodes[:, NT * C:2 * NT * C].rearrange("p (t c) -> p t c", c=C)
        tb_at = 2 * NT * C
        tb_h = nodes[:, tb_at:tb_at + NT * HID].rearrange("p (t c) -> p t c", c=HID)
        tb = nodes[:, tb_at:tb_at + NT * C].rearrange("p (t c) -> p t c", c=C)
        tb_att = nodes[:, tb_at:tb_at + NT * L3ROW].rearrange("p (t c) -> p t c", c=L3ROW)
        tilech = nodes[:, :].rearrange("p (c t) -> p c t", c=SCAL)
        xn = sb("xn", [P, NT, C])
        xc = sb("xc", [P, NT, C])
        loc = sb("loc", [P, ET])
        base = sb("base", [1, ET], I32)
        work = sb("work", [P, 11136])
        at = [0]

        def carve(words):
            at[0] += words
            assert at[0] <= 11136
            return work[:, at[0] - words:at[0]]

        gbuf = carve(2 * G * HID).rearrange("p (h n) -> p h n", h=2)
        oh = carve(2 * G * WIN).rearrange("p (h t j) -> p h t j", h=2, j=WIN)
        bs = carve(2 * G * BASIS).rearrange("p (h t k) -> p h t k", h=2, k=BASIS)
        u0 = carve(2 * SUB * P).rearrange("p (s t n) -> p s t n", s=2, n=P)
        ut = carve(2 * SUB * P).rearrange("p (s t n) -> p s t n", s=2, n=P)
        zb = carve(2 * 2 * K12 * C).rearrange("p (s t k c) -> p s t k c", s=2, t=2, c=C)
        msg = carve(2 * SUB * C).rearrange("p (s t c) -> p s t c", s=2, c=C)
        at[0] = 0
        stg = carve(2 * BN).rearrange("p (h n) -> p h n", h=2)
        hid = carve(2 * BN).rearrange("p (h n) -> p h n", h=2)
        xt = carve(2 * BN).rearrange("p (h n) -> p h n", h=2)
        stn = carve(2 * BT * C).rearrange("p (h t c) -> p h t c", h=2, c=C)
        sq = carve(NT * C).rearrange("p (t c) -> p t c", c=C)
        at[0] = 0
        pen_f, pen_b, pen_self, cont, t1, t2 = (carve(ET) for _ in range(6))
        attr = sb("attr", [P, 2, G, 3])
        hat = sb("hat", [P, G, 3, KS])
        bas = sb("bas", [P, 2, G, BASIS])

        ident = sb("ident", [P, P])
        ones = sb("ones", [P, P])
        iota_i = sb("iota_i", [P, P], I32)
        iota_f = sb("iota_f", [P, P])
        real = sb("real", [P, 1])
        epsc = sb("epsc", [P, 1])
        cnt = sb("cnt", [P, NT])
        dinv = sb("dinv", [P, NT])
        dinv2 = sb("dinv2", [P, NT])
        rcnt = sb("rcnt", [P, NT])
        stat = sb("stat", [P, NT])
        stat2 = sb("stat2", [P, NT])
        colsum = sb("colsum", [P, C])
        mean = sb("mean", [P, C])
        rstd = sb("rstd", [P, C])
        w1 = sb("w1", [C, HID])
        w2 = sb("w2", [HID, HID])
        w3 = sb("w3", [HID, HID])
        w4 = sb("w4", [HID, C])
        b1c = sb("b1c", [HID, 1])
        b2c = sb("b2c", [HID, 1])
        b3c = sb("b3c", [HID, 1])
        b2r = sb("b2r", [P, HID])
        b4r = sb("b4r", [P, C])
        wk = sb("wk", [P, 3, K12, C])
        rw = sb("rw", [C, 3, C])
        sbr = sb("sbr", [P, 3, C])
        sgr = sb("sgr", [P, 3, C])
        sber = sb("sber", [P, 3, C])
        wh = sb("wh", [P, C])
        whf = sb("whf", [C, HEADS, C])
        fcr = sb("fcr", [C, 2, C])
        fcb = sb("fcb", [P, 1])
        v8 = sb("v8", [C, SCAL])
        vtmp = sb("vtmp", [C, SCAL, C])
        abr = sb("abr", [P, C])
        idx = sb("idx", [P, 2, G], I32)
        car = sb("car", [P, SCAL])
        pen8 = sb("pen8", [P, SCAL])
        carr = sb("carr", [SCAL, P])
        penr = sb("penr", [SCAL, P])
        carry = sb("carry", [SCAL, P + 1])
        init = sb("init", [P, SCAL])

        ps = ctx.enter_context(nc.psum_tensor("ps", [P, 8, 512], F32))

        halves, subs = 2 * TURNS, 2 * TURNS * SUBS
        every = {p: subs for p in PASSES if p != "collect"}
        made_u = {p: subs for p in SPLINE + ["apply"]}
        onehot_ready = Signal(sem("onehot_ready"), {p: halves for p in PASSES if p != "collect"})
        sums_ready = Signal(sem("sums_ready"), every, lead=2 * SUBS)
        added = Signal(sem("added"), {p: ET for p in PASSES if p != "collect"}, lead=2 * SUB)
        u_ready = Signal(sem("u_ready"), made_u, lead=2 * SUBS)
        ut_ps = Signal(sem("ut_ps"), {p: subs for p in SPLINE}, lead=2)
        ut_ready = Signal(sem("ut_ready"), {p: subs for p in SPLINE}, lead=2)
        z_ready = Signal(sem("z_ready"), {p: 2 * subs for p in SPLINE}, lead=4)
        y_ready = Signal(sem("y_ready"), {p: 2 * subs for p in SPLINE}, lead=4 * SUBS)
        msg_ready = Signal(sem("msg_ready"), {p: 2 * subs for p in SPLINE})
        scal_copied = Signal(sem("scal_copied"), {"collect": halves}, lead=2)
        idx_in = [sem("idx_in0"), sem("idx_in1")]
        basis_in = [sem("basis_in0"), sem("basis_in1")]
        gathered = {p: [sem(f"got_{p}{h}") for h in range(2)] for p in TABLE}
        rows_in = [sem("rows_in0"), sem("rows_in1")]
        rows_out = [sem("rows_out0"), sem("rows_out1")]
        attr_in = [sem("attr_in0"), sem("attr_in1")]
        bas_ready = Signal(sem("bas_ready"), {"gin1": halves}, lead=2)
        turn_chain = sem("turn_chain")
        bas_out = [sem("bas_out0"), sem("bas_out1")]
        held = {k: sem(f"held_{k}") for k in ("pool", "act", "dve", "pe")}
        consts = sem("consts")
        loads = sem("loads")
        xload = sem("xload")
        chain = sem("chain")
        table_ready = sem("table_ready")
        ones_set = sem("ones_set")
        seg_in = sem("seg_in")
        stored = sem("stored")
        out_stored = sem("out_stored")

        NODE = ["gin1", "gin2", "gcn1", "gcn2", "sp1", "sp2", "sp3", "apply"]
        HIDDEN = ["gin1", "gin2"]
        staged = Signal(sem("staged"), {p: BLOCKS for p in NODE})
        hid_ps = Signal(sem("hid_ps"), {p: BLOCKS for p in HIDDEN})
        hid_ready = Signal(sem("hid_ready"), {p: BLOCKS for p in HIDDEN}, lead=1)
        out_ps = Signal(sem("out_ps"), {p: BLOCKS for p in NODE}, lead=2)
        out_done = Signal(sem("out_done"), {p: BLOCKS for p in NODE}, lead=2)
        fm_done = Signal(sem("fm_done"), {"gin1": BLOCKS}, lead=1)
        TURNED = ["x", "gin2", "gcn1", "sp1", "sp2", "sp3", "collect"]
        PROJ = ["sp1", "sp2", "sp3", "collect"]
        tstaged = Signal(sem("tstaged"), {p: BLOCKS for p in TURNED})
        turned_ps = Signal(sem("turned_ps"), {p: BLOCKS for p in TURNED}, lead=2)
        turned = Signal(sem("turned"), {p: BLOCKS for p in TURNED}, lead=2)
        proj_ps = Signal(sem("proj_ps"), {p: BLOCKS for p in PROJ}, lead=2)
        proj_done = Signal(sem("proj_done"), {p: BLOCKS for p in PROJ}, lead=2)
        to_pe = sem("to_pe")
        from_pe = sem("from_pe")
        to_act = sem("to_act")
        from_act = sem("from_act")
        cstaged = Signal(sem("cstaged"), {"rows": SCAL, "tiles": HEADS})
        cturn_ps = Signal(sem("cturn_ps"), {"rows": SCAL, "tiles": HEADS}, lead=2)
        cturned = Signal(sem("cturned"), {"rows": SCAL, "tiles": HEADS}, lead=1)

        LEADS = {"pe": [sums_ready, ut_ps, z_ready, out_ps, turned_ps, proj_ps, cturn_ps],
                 "dve": [added, u_ready, y_ready, bas_ready, out_done, proj_done],
                 "act": [ut_ready, hid_ready, fm_done, turned, cturned, scal_copied]}

        def lead_in(eng, name):
            for s in LEADS[name]:
                eng.sem_inc(s.sem, s.lead)

        def hold(eng, name, s, value):
            eng.wait_ge(s, value)
            eng.sem_inc(held[name], 1)


        def rows(p, h):
            w = {"gin1": C + 4, "apply": L3ROW}.get(p) or ROW[p]
            return gbuf[:, h, 0:G * w].rearrange("p (t c) -> p t c", c=w)

        def acc_rows(p):
            return {"gin1": C + 1, "gin2": HID, "apply": P}.get(p, C)

        def flat(bank, n, rows_=P):
            return ps[0:rows_, bank:bank + -(-n // 512), :].rearrange("p b n -> p (b n)")[:, 0:n]

        cst = [pen_f, pen_b]

        STORES = ["gin2", "gcn1", "gcn2", "sp1", "sp2", "sp3", "collect"]
        LOADS = []

        block = ctx.enter_context(nc.Block())

        @block.sync
        def _(sp):
            sp.dma_start(xn[:, :, :], x.rearrange("(t p) c -> p t c", p=P)).then_inc(xload, 16)
            LOADS.extend([
                (t1.bitcast(I32), dst_tile), (t2.bitcast(I32), dst_base.broadcast_to([P, ET])),
                (base[:, :], dst_base),
                (w1[:, :], gW1), (w2[:, :], gW2), (w3[:, :], gW3), (w4[:, :], gW4),
                (b1c[:, :], gb1.unsqueeze(1)), (b2c[:, :], gb2.unsqueeze(1)), (b3c[:, :], gb3.unsqueeze(1)),
                (b2r[:, :], gb2.partition_broadcast(P)), (b4r[:, :], gb4.partition_broadcast(P)),
                (wh[:, :], aw.rearrange("h f o -> (h f) o")), (whf[:, :, :], aw.rearrange("h f o -> f h o")),
                (fcr[:, :, :].rearrange("p s o -> p (s o)"), fc_w.broadcast_to([C, 2 * C])),
                (fcb[:, :], fc_b.partition_broadcast(P)), (abr[:, :], abias.partition_broadcast(P)),
            ])
            for l in range(3):
                for k0 in range(KS):
                    LOADS.append((wk[k0 * C:(k0 + 1) * C, l, :, :], sW[l].rearrange("(k m) c o -> m c k o", m=KS)[k0]))
                LOADS.append((rw[:, l, :], sR[l]))
                for dst, v in ((sbr, sb_), (sgr, sg), (sber, sbe)):
                    LOADS.append((dst[:, l, :], v[l].partition_broadcast(P)))
            for dst, src in LOADS:
                sp.dma_start(dst, src).then_inc(loads, 16)

            def store_table(p):
                n = STORES.index(p) + 1
                src = {"gin2": tb_h, "gcn1": tb, "gcn2": tb, "collect": tb_att}.get(p, xc[:, :, :])
                sp.wait_ge(table_ready, n)
                sp.dma_start(TABLE[p].rearrange("(t p) c -> p t c", p=P), src).then_inc(stored, 16)

            def index_loads(p):
                if p == "sp1":
                    for h in range(2):
                        sp.wait_ge(bas_out[h], 16 * TURNS)
                with sp.Fori(0, TURNS) as i:
                    for h in range(2):
                        k, tile0 = 2 * i + h, (2 * i + h) * G
                        if p != "apply":
                            sp.wait_ge(gathered[p][h], i * (16 * G))
                            sp.dma_start(idx[:, h, :], src_tile[:, bass.ds(tile0, G)]).then_inc(idx_in[h], 16)
                        if p == "gin1":
                            sp.wait_ge(bas_ready.sem, bas_ready.done(p, k - 2))
                            sp.dma_start(attr[:, h, :, :].rearrange("p t d -> p (t d)"),
                                         attr_tile[:, bass.ds(tile0 * 3, G * 3)]).then_inc(attr_in[h], 16)
                        if p in SPLINE:
                            sp.wait_ge(y_ready.sem, y_ready.done(p, 2 * SUBS * (k - 2) + 2 * SUBS - 1))
                            sp.dma_start(bs[:, h, :, :].rearrange("p t k -> p (t k)"),
                                         basis_d[:, bass.ds(tile0 * BASIS, G * BASIS)]).then_inc(basis_in[h], 16)
                        if p == "apply":
                            sp.wait_ge(u_ready.sem, u_ready.done(p, SUBS * (k - 2) + SUBS - 1))
                            sp.dma_start(gbuf[:, h, 0:G * L3ROW],
                                         edge_rows[:, bass.ds(tile0 * L3ROW, G * L3ROW)]).then_inc(rows_in[h], 16)

            index_loads("gin1")
            for p in PASSES[1:-1]:
                store_table(p)
                index_loads(p)
            sp.wait_ge(scal_copied.sem, scal_copied.done("collect", halves - 1))
            for dst, src in ((t1, dst_ext[1:1 + P * ET]), (t2, dst_ext[0:P * ET]),
                             (cont, dst_ext[2:2 + P * ET])):
                sp.dma_start(dst.bitcast(I32), src.rearrange("(p e) -> p e", p=P)).then_inc(seg_in, 16)
            sp.dma_start(pen_self.bitcast(I32), src_row).then_inc(seg_in, 16)
            for h in range(2):
                sp.wait_ge(rows_out[h], 16 * TURNS)
            sp.wait_ge(table_ready, len(STORES) + 1)
            index_loads("apply")
            sp.wait_ge(table_ready, len(STORES) + 2)
            full = NT - 1
            sp.dma_start(out[0:full * P, :].rearrange("(t p) c -> p t c", p=P), xn[:, 0:full, :]).then_inc(out_stored, 16)
            sp.dma_start(out[full * P:N, :], xn[0:LAST_ROWS, full, :]).then_inc(out_stored, 16)
            sp.wait_ge(out_stored, 32)

        @block.gpsimd
        def _(pool):
            pool.memset(ones[:, :], 1.0).then_inc(consts, 1)
            pool.memset(ident[:, :], 0.0).then_inc(consts, 1)
            pool.memset(real[:, :], 1.0).then_inc(consts, 1)
            pool.iota(iota_i[:, :], pattern=[[1, P]], base=0, channel_multiplier=0).then_inc(consts, 1)
            pool.wait_ge(consts, 4)
            pool.affine_select(out=ident[:, :], in_=ident[:, :], compare_op=ALU.not_equal, fill=1.0, base=0,
                               pattern=[[-1, P]], channel_multiplier=1).then_inc(consts, 1)
            pool.affine_select(out=real[:, :], in_=real[:, :], compare_op=ALU.is_ge, fill=0.0,
                               base=LAST_ROWS - 1, pattern=[[0, 1]], channel_multiplier=-1).then_inc(consts, 1)

            def gathers(p):
                if p != "gin1":
                    hold(pool, "pool", stored, 16 * (STORES.index(p) + 1))
                else:
                    hold(pool, "pool", ones_set, 1)
                with pool.Fori(0, TURNS) as i:
                    for h in range(2):
                        k = 2 * i + h
                        if p in SPLINE:
                            hold(pool, "pool", u_ready.sem, u_ready.done(p, SUBS * (k - 2) + SUBS - 1))
                        elif p == "collect":
                            hold(pool, "pool", scal_copied.sem, scal_copied.done(p, k - 2))
                            hold(pool, "pool", rows_out[h], 16 * i)
                        else:
                            hold(pool, "pool", sums_ready.sem, sums_ready.done(p, SUBS * (k - 2) + SUBS - 1))
                        hold(pool, "pool", idx_in[h], (i + 1) * 16 + 16 * TURNS * PASSES.index(p))
                        for t in range(G):
                            pool.indirect_dma_start(
                                out=rows(p, h)[:, t, 0:ROW[p]], out_offset=None, in_=TABLE[p],
                                in_offset=bass.IndirectOffsetOnAxis(ap=idx[:, h, t:t + 1], axis=0),
                            ).then_inc(gathered[p][h], 16)

            for p in PASSES[:-1]:
                gathers(p)

        @block.tensor
        def _(pe):
            lead_in(pe, "pe")
            asked = [0]

            def answer(emit):
                asked[0] += 1
                pe.wait_ge(to_pe, asked[0])
                emit().then_inc(from_pe, 1)

            def window_sums(p, k, h, s, rhs_row):
                g = SUBS * k + s
                pe.wait_ge(added.sem, added.done(p, SUB * (g - 2) + SUB - 1))
                for q in range(SUB):
                    m = acc_rows(p)
                    last = nc.tensor.matmul(ps[0:m, 6 + s % 2, q * WIN:(q + 1) * WIN], rhs_row(q),
                                            oh[:, h, s * SUB + q, :], start=True, stop=True)
                last.then_inc(sums_ready.sem, 1)

            def turns_of_rows(p, k, s):
                g = SUBS * k + s
                hold(pe, "pe", u_ready.sem, u_ready.done(p, g))
                pe.wait_ge(ut_ready.sem, ut_ready.done(p, g - 2))
                for q in range(SUB):
                    last = nc.tensor.transpose(ps[:, s % 2, q * P:(q + 1) * P], u0[:, s % 2, q, :], ident[:, :])
                last.then_inc(ut_ps.sem, 1)

            def kernels_product(p, k, s, half):
                u = 2 * (SUBS * k + s) + half
                hold(pe, "pe", ut_ready.sem, ut_ready.done(p, SUBS * k + s))
                pe.wait_ge(y_ready.sem, y_ready.done(p, u - 2))
                for q in range(2):
                    last = nc.tensor.matmul(ps[:, 2 + 2 * half + q, :], ut[:, s % 2, 2 * half + q, :],
                                            wk[:, SPLINE.index(p), :, :].rearrange("p k c -> p (k c)"),
                                            start=True, stop=True)
                last.then_inc(z_ready.sem, 1)

            def message_sums(p, k, h, s):
                hold(pe, "pe", msg_ready.sem, msg_ready.done(p, 2 * (SUBS * k + s) + 1))
                window_sums(p, k, h, s, lambda q: msg[:, s % 2, q, :])

            def edge_pass(p):
                with pe.Fori(0, TURNS) as i:
                    for h in range(2):
                        k = 2 * i + h
                        hold(pe, "pe", onehot_ready.sem, onehot_ready.done(p, k))
                        if p in SPLINE:
                            turns_of_rows(p, k, 0)
                            turns_of_rows(p, k, 1)
                            for s in range(SUBS):
                                kernels_product(p, k, s, 0)
                                kernels_product(p, k, s, 1)
                                if s >= 1:
                                    message_sums(p, k, h, s - 1)
                                    if s + 1 < SUBS:
                                        turns_of_rows(p, k, s + 1)
                            message_sums(p, k, h, SUBS - 1)
                        elif p == "apply":
                            for s in range(SUBS):
                                hold(pe, "pe", u_ready.sem, u_ready.done(p, SUBS * k + s))
                                window_sums(p, k, h, s, lambda q: u0[:, s % 2, q, :])
                        else:
                            hold(pe, "pe", gathered[p][h], (i + 1) * (16 * G))
                            for s in range(SUBS):
                                window_sums(p, k, h, s, lambda q: rows(p, h)[:, s * SUB + q, 0:acc_rows(p)])

            def turn(name):
                proj = {"sp1": rw[:, 0, :], "sp2": rw[:, 1, :], "sp3": rw[:, 2, :], "collect": v8[:, :]}.get(name)
                with pe.Fori(0, BLOCKS // 2) as i:
                    for h in range(2):
                        b = 2 * i + h
                        hold(pe, "pe", tstaged.sem, tstaged.done(name, b))
                        pe.wait_ge(turned.sem, turned.done(name, b - 2))
                        for j in range(BT):
                            last = nc.tensor.matmul(flat(2 * h, BN, C)[:, j * P:(j + 1) * P], stn[:, h, j, :],
                                                    ident[:, :], start=True, stop=True)
                        last.then_inc(turned_ps.sem, 1)
                    if proj is not None:
                        for h in range(2):
                            b, w = 2 * i + h, proj.shape[-1]
                            hold(pe, "pe", turned.sem, turned.done(name, b))
                            pe.wait_ge(proj_done.sem, proj_done.done(name, b - 2))
                            for j in range(BT):
                                last = nc.tensor.matmul(ps[:, 4 + h, j * w:(j + 1) * w],
                                                        xt[0:C, h, j * P:(j + 1) * P], proj, start=True, stop=True)
                            last.then_inc(proj_ps.sem, 1)

            def node_phase(p):
                first, bank = {"gin1": (w1, 0), "gin2": (w3, 0)}.get(p), None
                second = {"gin1": w2[:, :], "gin2": w4[:, :], "apply": wh[:, :]}.get(p, ident[0:C, 0:C])
                w = second.shape[-1]
                m = {"gin1": HID, "gin2": HID, "apply": P}.get(p, C)
                with pe.Fori(0, BLOCKS // 2) as i:
                    if first is not None:
                        for h in range(2):
                            b = 2 * i + h
                            hold(pe, "pe", staged.sem, staged.done(p, b))
                            hold(pe, "pe", hid_ready.sem, hid_ready.done(p, b - 1))
                            kk = C if p == "gin1" else HID
                            for c0, c1 in ((0, 512), (512, BN)):
                                last = nc.tensor.matmul(flat(0, BN, HID)[:, c0:c1], first[0][:, :],
                                                        stg[0:kk, h, c0:c1], start=True, stop=True)
                            last.then_inc(hid_ps.sem, 1)
                    for h in range(2):
                        b = 2 * i + h
                        if first is not None:
                            hold(pe, "pe", hid_ready.sem, hid_ready.done(p, b))
                        else:
                            hold(pe, "pe", staged.sem, staged.done(p, b))
                        src = hid if first is not None else stg
                        pe.wait_ge(out_done.sem, out_done.done(p, b - 2))
                        if p == "gin1":
                            hold(pe, "pe", fm_done.sem, fm_done.done(p, b - 1))
                            for c0, c1 in ((0, 512), (512, BN)):
                                nc.tensor.matmul(flat(2, BN, HID)[:, c0:c1], w2[:, :], hid[0:HID, h, c0:c1],
                                                 start=True, stop=True)
                            for j in range(BT):
                                nc.tensor.matmul(ps[:, 6 + h, j:j + 1], stg[C:C + 1, h, j * P:(j + 1) * P],
                                                 ones[C:C + 1, 0:1], start=True, stop=True)
                        for j in range(BT):
                            last = nc.tensor.matmul(ps[:, 4 + h, j * w:(j + 1) * w], src[0:m, h, j * P:(j + 1) * P],
                                                    second, start=True, stop=True)
                        last.then_inc(out_ps.sem, 1)

            def col_sums():
                answer(lambda: nc.tensor.matmul(ps[:, 7, 0:C], ones[:, :], colsum[:, :], start=True, stop=True))

            def chunk_turns(name, n):
                with pe.Fori(0, n // 2) as i:
                    for h in range(2):
                        c = 2 * i + h
                        hold(pe, "pe", cstaged.sem, cstaged.done(name, c))
                        pe.wait_ge(cturned.sem, cturned.done(name, c - 1))
                        for r in range(RCH):
                            last = nc.tensor.transpose(flat(0, ET)[:, r * P:(r + 1) * P],
                                                       cst[h][:, r * P:(r + 1) * P], ident[:, :])
                        last.then_inc(cturn_ps.sem, 1)

            pe.wait_ge(consts, 6)
            pe.wait_ge(loads, 16 * len(LOADS))
            turn("x")
            edge_pass("gin1")
            node_phase("gin1")
            edge_pass("gin2")
            node_phase("gin2")
            turn("gin2")
            edge_pass("gcn1")
            node_phase("gcn1")
            turn("gcn1")
            edge_pass("gcn2")
            node_phase("gcn2")
            for p in SPLINE:
                turn(p)
                edge_pass(p)
                node_phase(p)
                col_sums()
                col_sums()
            turn("collect")
            chunk_turns("rows", SCAL)
            for carry_in in (carry[:, 0:P], carry[:, 1:P + 1]) * 2:
                answer(lambda: nc.tensor.transpose(ps[0:SCAL, 5, 0:P], car[:, :], ident[:, :]))
                answer(lambda: nc.tensor.transpose(ps[0:SCAL, 5, P:2 * P], pen8[:, :], ident[:, :]))
                answer(lambda: nc.tensor.transpose(ps[:, 6, 0:SCAL], carry_in, ident[0:SCAL, 0:SCAL]))
            chunk_turns("tiles", HEADS)
            edge_pass("apply")
            node_phase("apply")

        @block.scalar
        def _(act):
            lead_in(act, "act")
            asked = [0]

            def answer(emit):
                asked[0] += 1
                act.wait_ge(to_act, asked[0])
                emit().then_inc(from_act, 1)

            def root(n):
                if n == C:
                    answer(lambda: nc.scalar.activation(stat2[:, :], stat[:, :], ACT.Sqrt, bias=epsc[:, :], scale=1.0 / C))
                else:
                    answer(lambda: nc.scalar.activation(mean[:, :], ps[:, 7, 0:C], ACT.Sqrt, bias=epsc[:, :], scale=1.0 / N))

            def turn(name):
                with act.Fori(0, BLOCKS // 2) as i:
                    for h in range(2):
                        b = 2 * i + h
                        hold(act, "act", turned_ps.sem, turned_ps.done(name, b))
                        if name in PROJ:
                            hold(act, "act", proj_ps.sem, proj_ps.done(name, b - 2))
                            dst = xt[0:C, h, :]
                        else:
                            dst = acc[0:C, bass.ds(b * BN, BN)]
                        nc.scalar.activation(dst, flat(2 * h, BN, C), ACT.Copy).then_inc(turned.sem, 1)

            def hidden(p):
                bias = {"gin1": b1c, "gin2": b3c}[p]
                with act.Fori(0, BLOCKS // 2) as i:
                    for h in range(2):
                        b = 2 * i + h
                        hold(act, "act", hid_ps.sem, hid_ps.done(p, b))
                        hold(act, "act", out_ps.sem, out_ps.done(p, b - 2))
                        nc.scalar.activation(hid[0:HID, h, :], flat(0, BN, HID), ACT.Relu,
                                             bias=bias[:, :]).then_inc(hid_ready.sem, 1)
                    for h in range(2):
                        b = 2 * i + h
                        if p == "gin1":
                            hold(act, "act", out_ps.sem, out_ps.done(p, b))
                            nc.scalar.activation(acc[0:HID, bass.ds(b * BN, BN)], flat(2, BN, HID), ACT.Relu,
                                                 bias=b2c[:, :]).then_inc(fm_done.sem, 1)

            def store_basis():
                with act.Fori(0, TURNS) as i:
                    for h in range(2):
                        k = 2 * i + h
                        act.wait_ge(bas_ready.sem, bas_ready.done("gin1", k))
                        act.dma_start(basis_d[:, bass.ds(k * (G * BASIS), G * BASIS)],
                                      bas[:, h, :, :].rearrange("p t k -> p (t k)")).then_inc(bas_out[h], 16)

            def copy_turned_rows(p):
                with act.Fori(0, TURNS) as i:
                    for h in range(2):
                        for s in range(SUBS):
                            g = SUBS * (2 * i + h) + s
                            hold(act, "act", ut_ps.sem, ut_ps.done(p, g))
                            act.wait_ge(z_ready.sem, z_ready.done(p, 2 * (g - 2) + 1))
                            nc.scalar.activation(ut[:, s % 2, :, :].rearrange("p t n -> p (t n)"), ps[:, s % 2, :],
                                                 ACT.Copy).then_inc(ut_ready.sem, 1)

            def collect():
                with act.Fori(0, TURNS) as i:
                    for h in range(2):
                        k = 2 * i + h
                        hold(act, "act", gathered["collect"][h], (i + 1) * (16 * G))
                        act.dma_start(edge_rows[:, bass.ds(k * (G * L3ROW), G * L3ROW)],
                                      gbuf[:, h, 0:G * L3ROW]).then_inc(rows_out[h], 16)
                        nc.scalar.activation(tilech[:, :, bass.ds(k * G, G)],
                                             rows("collect", h)[:, :, C:L3ROW].rearrange("p t c -> p c t"),
                                             ACT.Copy).then_inc(scal_copied.sem, 1)

            def chunk_turns(name, n):
                with act.Fori(0, n // 2) as i:
                    for h in range(2):
                        c = 2 * i + h
                        hold(act, "act", cturn_ps.sem, cturn_ps.done(name, c))
                        src = flat(0, ET)
                        if name == "rows":
                            dst = big[:, bass.ds(c * ET, ET)]
                        else:
                            src = src.rearrange("p (r q) -> p r q", r=RCH)
                            dst = nodes[:, bass.ds(c * ET, ET)].rearrange("p (q r) -> p r q", r=RCH)
                        nc.scalar.activation(dst, src, ACT.Copy).then_inc(cturned.sem, 1)

            act.wait_ge(loads, 16 * len(LOADS))
            turn("x")
            store_basis()
            hidden("gin1")
            hidden("gin2")
            root(C)
            answer(lambda: nc.scalar.activation(stat[:, :], dinv2[:, :], ACT.Sqrt))
            turn("gin2")
            turn("gcn1")
            root(C)
            for p in SPLINE:
                turn(p)
                copy_turned_rows(p)
                root(N)
            root(C)
            turn("collect")
            collect()
            chunk_turns("rows", SCAL)
            heads = big[:, 0:HEADS * ET]
            answer(lambda: nc.scalar.activation(heads, heads, ACT.Exp))
            chunk_turns("tiles", HEADS)
            root(C)

        @block.vector
        def _(dve):
            lead_in(dve, "dve")
            count, turn_base, to_act_n, to_pe_n = [0], [0], [0], [0]
            regs = [dve.alloc_register(f"first{t}") for t in range(G)]
            v = nc.vector

            def link(ins):
                count[0] += 1
                ins.then_inc(chain, 1)
                dve.wait_ge(chain, count[0])

            class TurnLink:

                def __init__(self, i, n):
                    self.i, self.n, self.k = i, n, 0

                def __call__(self, ins):
                    self.k += 1
                    assert self.k <= self.n
                    ins.then_inc(turn_chain, 1)
                    dve.wait_ge(turn_chain, self.i * self.n + (turn_base[0] + self.k))

                def close(self, turns):
                    assert self.k == self.n
                    turn_base[0] += self.n * turns

            def ask_act(ins):
                to_act_n[0] += 1
                ins.then_inc(to_act, 1)
                dve.wait_ge(from_act, to_act_n[0])

            def ask_pe(ins):
                to_pe_n[0] += 1
                ins.then_inc(to_pe, 1)
                dve.wait_ge(from_pe, to_pe_n[0])

            def over_tiles(row):
                return row.unsqueeze(1).broadcast_to([P, NT, C])

            def over_features(col, n=NT):
                return col.unsqueeze(2).broadcast_to([P, n, C])

            def layer_norm():
                link(v.tensor_reduce(stat[:, :], yn, axis=AX.X, op=ALU.add))
                link(v.tensor_scalar(stat[:, :], stat[:, :], 1.0 / C, None, ALU.mult))
                link(v.tensor_tensor(yn, yn, over_features(stat[:, :]), ALU.subtract))
                link(v.tensor_tensor(sq, yn, yn, ALU.mult))
                ask_act(v.tensor_reduce(stat[:, :], sq, axis=AX.X, op=ALU.add))
                link(v.reciprocal(stat[:, :], stat2[:, :]))
                link(v.tensor_tensor(xn[:, :, :], yn, over_features(stat[:, :]), ALU.mult))

            def batch_norm(l):
                last, cols = NT - 1, (lambda a: a.rearrange("p t c -> p c t"))
                link(v.tensor_scalar(yn[:, last, :], yn[:, last, :], real[:, :], None, ALU.mult))
                ask_pe(v.tensor_reduce(colsum[:, :], cols(yn), axis=AX.X, op=ALU.add))
                link(v.tensor_scalar(mean[:, :], ps[:, 7, 0:C], 1.0 / N, None, ALU.mult))
                link(v.tensor_tensor(yn, yn, over_tiles(mean[:, :]), ALU.subtract))
                link(v.tensor_scalar(yn[:, last, :], yn[:, last, :], real[:, :], None, ALU.mult))
                link(v.tensor_tensor(sq, yn, yn, ALU.mult))
                ask_pe(v.tensor_reduce(colsum[:, :], cols(sq), axis=AX.X, op=ALU.add))
                ask_act(v.tensor_scalar(stat[:, 0:1], epsc[:, :], 1.0, None, ALU.mult))
                link(v.reciprocal(rstd[:, :], mean[:, :]))
                link(v.tensor_tensor(rstd[:, :], rstd[:, :], sgr[:, l, :], ALU.mult))
                link(v.tensor_tensor(yn, yn, over_tiles(rstd[:, :]), ALU.mult))
                link(v.tensor_tensor(xc[:, :, :], yn, over_tiles(sber[:, l, :]), ALU.add))

            def turn(name):
                src = {"x": xn[:, :, :], "gin2": tb, "gcn1": tb, "collect": xn[:, :, :]}.get(name, xc[:, :, :])
                with dve.Fori(0, BLOCKS // 2) as i:
                    for h in range(2):
                        b = 2 * i + h
                        hold(dve, "dve", turned_ps.sem, turned_ps.done(name, b - 2))
                        v.tensor_copy(stn[:, h, :, :], src[:, bass.ds(b * BT, BT), :]).then_inc(tstaged.sem, 1)
                    if name in PROJ:
                        for h in range(2):
                            b = 2 * i + h
                            dve.wait_ge(proj_ps.sem, proj_ps.done(name, b))
                            if name == "collect":
                                got = ps[:, 4 + h, 0:BT * SCAL].rearrange("p (t c) -> p t c", c=SCAL)
                                ins = v.tensor_scalar(tb_att[:, bass.ds(b * BT, BT), C:L3ROW], got, 1.0, None, ALU.mult)
                            else:
                                got = ps[:, 4 + h, 0:BT * C].rearrange("p (t c) -> p t c", c=C)
                                bias = sbr[:, SPLINE.index(name), :].unsqueeze(1).broadcast_to([P, BT, C])
                                ins = v.tensor_tensor(rn[:, bass.ds(b * BT, BT), :], got, bias, ALU.add)
                            ins.then_inc(proj_done.sem, 1)
                if name in PROJ:
                    dve.wait_ge(proj_done.sem, proj_done.done(name, BLOCKS - 1))
                else:
                    dve.wait_ge(turned.sem, turned.done(name, BLOCKS - 1))

            def node_phase(p):
                kk = acc_rows(p)
                dve.wait_ge(added.sem, added.done(p, ET - 1))
                with dve.Fori(0, BLOCKS // 2) as i:
                    for h in range(2):
                        b = 2 * i + h
                        hold(dve, "dve", out_ps.sem, out_ps.done(p, b - 2))
                        v.tensor_copy(stg[0:kk, h, :], acc[0:kk, bass.ds(b * BN, BN)]).then_inc(staged.sem, 1)
                    for h in range(2):
                        b = 2 * i + h
                        tiles = bass.ds(b * BT, BT)
                        dve.wait_ge(out_ps.sem, out_ps.done(p, b))
                        w = HID if p == "gin1" else C
                        got = ps[:, 4 + h, 0:BT * w].rearrange("p (t c) -> p t c", c=w)
                        if p == "gin1":
                            v.tensor_tensor(tb_h[:, tiles, :], got, b2r[:, :].unsqueeze(1).broadcast_to([P, BT, HID]), ALU.add)
                            ins = v.tensor_copy(cnt[:, tiles], ps[:, 6 + h, 0:BT])
                        elif p == "gin2":
                            ins = v.tensor_tensor(yn[:, tiles, :], got, b4r[:, :].unsqueeze(1).broadcast_to([P, BT, C]), ALU.add)
                        elif p == "apply":
                            ins = v.scalar_tensor_tensor(yn[:, tiles, :], got, 1.0 / HEADS,
                                                         abr[:, :].unsqueeze(1).broadcast_to([P, BT, C]), ALU.mult, ALU.add)
                        else:
                            scale, dst = {"gcn1": (dinv2, tb), "gcn2": (dinv, yn)}.get(p, (rcnt, yn))
                            ins = v.tensor_tensor(dst[:, tiles, :], got, over_features(scale[:, tiles], BT), ALU.mult)
                        ins.then_inc(out_done.sem, 1)
                dve.wait_ge(out_done.sem, out_done.done(p, BLOCKS - 1))

            def make_basis(tl, i, h):
                hold(dve, "dve", attr_in[h], (i + 1) * 16)
                hold(dve, "dve", bas_out[h], i * 16)
                a = attr[:, h, :, :]
                link_ = tl
                link_(v.tensor_scalar(a, a, float(KS - 1), float(KS - 1), ALU.mult, ALU.min))
                flat_hat = hat[:, :, :, :].rearrange("p t d k -> p (t d) k")
                link_(v.scalar_tensor_tensor(flat_hat, a.rearrange("p t d -> p (t d)").unsqueeze(2).broadcast_to([P, 3 * G, KS]),
                                             0.0, iota_f[:, 0:KS].unsqueeze(1).broadcast_to([P, 3 * G, KS]),
                                             ALU.max, ALU.subtract))
                link_(v.scalar_tensor_tensor(flat_hat, flat_hat, -1.0, flat_hat, ALU.mult, ALU.min))
                link_(v.tensor_scalar(flat_hat, flat_hat, 1.0, 0.0, ALU.add, ALU.max))
                v.tensor_copy(bas[:, h, :, 0:KS], hat[:, :, 0, :])
                v.tensor_tensor(bas[:, h, :, KS:].rearrange("p t (a b) -> p t a b", b=KS),
                                hat[:, :, 2, :].unsqueeze(3).broadcast_to([P, G, KS, KS]),
                                hat[:, :, 1, :].unsqueeze(2).broadcast_to([P, G, KS, KS]), ALU.mult).then_inc(bas_ready.sem, 1)

            def one_hots(p, k, h):
                hold(dve, "dve", sums_ready.sem, sums_ready.done(p, SUBS * (k - 2) + SUBS - 1))
                v.tensor_tensor(oh[:, h, :, :], iota_f[:, :].unsqueeze(1).broadcast_to([P, G, WIN]),
                                loc[:, bass.ds(k * G, G)].unsqueeze(2).broadcast_to([P, G, WIN]),
                                ALU.is_equal).then_inc(onehot_ready.sem, 1)

            def add_windows(p, k, s, firsts):
                m, g = acc_rows(p), SUBS * k + s
                hold(dve, "dve", sums_ready.sem, sums_ready.done(p, g))
                for q in range(SUB):
                    window = acc[0:m, bass.ds(firsts[s * SUB + q], WIN)]
                    dve.wait_ge(added.sem, added.done(p, SUB * g + q - 1))
                    v.tensor_tensor(window, window, ps[0:m, 6 + s % 2, q * WIN:(q + 1) * WIN], ALU.add)\
                     .then_inc(added.sem, 1)

            def weight_rows(p, k, h, s):
                g, t0 = SUBS * k + s, s * SUB
                if p == "apply":
                    hold(dve, "dve", sums_ready.sem, sums_ready.done(p, g - 2))
                    wts = tilech[:, 0:HEADS, bass.ds(k * G + t0, SUB)].rearrange("p h t -> p t h")
                else:
                    hold(dve, "dve", ut_ps.sem, ut_ps.done(p, g - 2))
                    wts = bs[:, h, t0:t0 + SUB, 0:KS]
                v.tensor_tensor(u0[:, s % 2, :, :].rearrange("p t (a c) -> p t a c", c=C),
                                rows(p, h)[:, t0:t0 + SUB, 0:C].unsqueeze(2).broadcast_to([P, SUB, 4, C]),
                                wts.unsqueeze(3).broadcast_to([P, SUB, 4, C]), ALU.mult).then_inc(u_ready.sem, 1)

            def messages(p, k, h, s, half, tl):
                u, t0 = 2 * (SUBS * k + s) + half, s * SUB + 2 * half
                z = ps[:, 2 + 2 * half:4 + 2 * half, :].rearrange("p t (k c) -> p t k c", c=C)
                dve.wait_ge(z_ready.sem, z_ready.done(p, u))
                v.tensor_tensor(zb[:, half, :, :, :], z,
                                bs[:, h, t0:t0 + 2, KS:].unsqueeze(3).broadcast_to([P, 2, K12, C]),
                                ALU.mult).then_inc(y_ready.sem, 1)
                dve.wait_ge(y_ready.sem, y_ready.done(p, u))
                v.tensor_reduce(msg[:, s % 2, 2 * half:2 * half + 2, :],
                                zb[:, half, :, :, :].rearrange("p t k c -> p t c k"),
                                axis=AX.X, op=ALU.add).then_inc(msg_ready.sem, 1)

            def edge_pass(p):
                with dve.Fori(0, TURNS) as i:
                    tl = TurnLink(i, 8) if p == "gin1" else None
                    for h in range(2):
                        k = 2 * i + h
                        dve.load(regs, base[0:1, bass.ds(k * G, G)])
                        firsts = [dve.snap(r, min_val=0, max_val=N) for r in regs]
                        if p in SPLINE:
                            hold(dve, "dve", gathered[p][h], (i + 1) * (16 * G))
                            hold(dve, "dve", basis_in[h], (i + 1) * 16 + 16 * TURNS * SPLINE.index(p))
                            weight_rows(p, k, h, 0)
                            weight_rows(p, k, h, 1)
                            one_hots(p, k, h)
                            for s in range(SUBS):
                                messages(p, k, h, s, 0, tl)
                                messages(p, k, h, s, 1, tl)
                                if s + 2 < SUBS:
                                    weight_rows(p, k, h, s + 2)
                                if s >= 1:
                                    add_windows(p, k, s - 1, firsts)
                            add_windows(p, k, SUBS - 1, firsts)
                        elif p == "apply":
                            one_hots(p, k, h)
                            hold(dve, "dve", rows_in[h], (i + 1) * 16)
                            weight_rows(p, k, h, 0)
                            weight_rows(p, k, h, 1)
                            for s in range(SUBS):
                                add_windows(p, k, s, firsts)
                                if s + 2 < SUBS:
                                    weight_rows(p, k, h, s + 2)
                        else:
                            one_hots(p, k, h)
                            if p == "gin1":
                                make_basis(tl, i, h)
                            for s in range(SUBS):
                                add_windows(p, k, s, firsts)
                if p == "gin1":
                    tl.close(TURNS)

            def chunk_turns(name, n):
                with dve.Fori(0, n // 2) as i:
                    for h in range(2):
                        c = 2 * i + h
                        hold(dve, "dve", cturn_ps.sem, cturn_ps.done(name, c - 2))
                        if name == "rows":
                            src = nodes[:, bass.ds(c * ET, ET)].rearrange("p (q r) -> p r q", r=RCH)
                        else:
                            src = big[:, bass.ds(c * ET, ET)].rearrange("p (r q) -> p r q", r=RCH)
                        v.tensor_copy(cst[h].rearrange("p (r q) -> p r q", r=RCH), src).then_inc(cstaged.sem, 1)
                dve.wait_ge(cturned.sem, cturned.done(name, n - 1))

            def scan_rows(chans, op0, op1, penalty, neutral, backward):
                way = (lambda a: a[:, ::-1]) if backward else (lambda a: a)
                end = 0 if backward else ET - 1
                for c, (dst, src) in enumerate(chans):
                    link(v.tensor_tensor_scan(t1, way(penalty), way(src), neutral, op0, op1))
                    link(v.tensor_copy(car[:, c:c + 1], t1[:, ET - 1:ET]))
                link(v.tensor_reduce(pen8[:, 0:1], penalty, axis=AX.X, op=ALU.min))
                link(v.tensor_copy(pen8[:, 1:SCAL], pen8[:, 0:1].broadcast_to([P, SCAL - 1])))
                ask_pe(v.tensor_copy(car[:, :], car[:, :]))
                link(v.tensor_copy(carr[:, :], ps[0:SCAL, 5, 0:P]))
                ask_pe(v.tensor_copy(pen8[:, :], pen8[:, :]))
                link(v.tensor_copy(penr[:, :], ps[0:SCAL, 5, P:2 * P]))
                edge, dst = (P, carry[:, 0:P]) if backward else (0, carry[:, 1:P + 1])
                link(v.memset(carry[:, edge:edge + 1], neutral))
                ask_pe(v.tensor_tensor_scan(way(dst), way(penr[:, :]), way(carr[:, :]), neutral, op0, op1))
                link(v.tensor_copy(init[:, :], ps[:, 6, 0:SCAL]))
                for c, (dst, src) in enumerate(chans):
                    link(v.tensor_tensor_scan(way(dst), way(penalty), way(src), init[:, c:c + 1], op0, op1))

            def attention():
                seg = nodes[:, 0:HEADS * ET]
                segch = [nodes[:, c * ET:(c + 1) * ET] for c in range(HEADS)]
                d = [rowch[:, c, :] for c in range(HEADS)]
                s = [rowch[:, HEADS + c, :] for c in range(HEADS)]
                dall, sall = big[:, 0:HEADS * ET], big[:, HEADS * ET:2 * HEADS * ET]
                dve.wait_ge(seg_in, 16 * 4)
                cur, prev, nxt, srcs = (a.bitcast(I32) for a in (t1, t2, cont, pen_self))
                link(v.tensor_tensor(pen_f, cur, prev, ALU.not_equal))
                link(v.tensor_scalar(pen_f, pen_f, -BIG, None, ALU.mult))
                link(v.tensor_tensor(pen_b, cur, nxt, ALU.not_equal))
                link(v.tensor_scalar(pen_b, pen_b, -BIG, None, ALU.mult))
                link(v.tensor_tensor(t2, cur, srcs, ALU.not_equal))
                link(v.tensor_scalar(t2, t2, -BIG, None, ALU.mult))
                for c in range(HEADS):
                    link(v.scalar_tensor_tensor(s[c], s[c], fcb[:, :], t2, ALU.add, ALU.add))
                up = [(segch[c], d[c]) for c in range(HEADS)] + [(s[c], s[c]) for c in range(HEADS)]
                down = [(o, o) for o, _ in up]
                scan_rows(up, ALU.add, ALU.max, pen_f, -BIG, False)
                scan_rows(down, ALU.add, ALU.max, pen_b, -BIG, True)
                link(v.tensor_tensor(dall, dall, sall, ALU.add))
                link(v.scalar_tensor_tensor(dall, dall, 0.2, dall, ALU.mult, ALU.max))
                link(v.tensor_tensor(seg, seg, sall, ALU.add))
                link(v.scalar_tensor_tensor(seg, seg, 0.2, seg, ALU.mult, ALU.max))
                ask_act(v.tensor_tensor(dall, dall, seg, ALU.subtract))
                link(v.tensor_tensor(cont, pen_f, pen_f, ALU.is_equal))
                link(v.tensor_scalar(cont, pen_f, 0.0, None, ALU.is_equal))
                up = [(segch[c], d[c]) for c in range(HEADS)]
                scan_rows(up, ALU.mult, ALU.add, cont, 0.0, False)
                scan_rows([(o, o) for o, _ in up], ALU.add, ALU.max, pen_b, -BIG, True)
                link(v.reciprocal(seg, seg))
                link(v.tensor_tensor(dall, dall, seg, ALU.mult))

            def table():
                link(v.tensor_copy(stat[:, 0:1], epsc[:, :]))
                dve.sem_inc(table_ready, 1)

            dve.wait_ge(consts, 6)
            dve.wait_ge(loads, 16 * len(LOADS))
            dve.wait_ge(xload, 16)
            link(v.memset(acc[:, :], 0.0))
            link(v.memset(epsc[:, :], EPS))
            link(v.memset(car[:, :], 0.0))
            link(v.tensor_copy(iota_f[:, :], iota_i[:, :]))
            link(v.tensor_tensor(loc[:, :], t1.bitcast(I32), t2.bitcast(I32), ALU.subtract))
            for which in range(2):
                part = vtmp[:, which * HEADS:(which + 1) * HEADS, :]
                link(v.tensor_tensor(part, whf[:, :, :], fcr[:, 1 - which, :].unsqueeze(1).broadcast_to([C, HEADS, C]), ALU.mult))
            link(v.tensor_reduce(v8[:, :], vtmp[:, :, :], axis=AX.X, op=ALU.add))
            for h in range(2):
                link(v.memset(rows("gin1", h)[:, :, C:], 1.0))
            dve.sem_inc(ones_set, 1)
            turn("x")

            edge_pass("gin1")
            node_phase("gin1")
            link(v.tensor_scalar(tb_h, tb_h, 0.0, None, ALU.max))
            table()
            dve.wait_ge(fm_done.sem, fm_done.done("gin1", BLOCKS - 1))
            link(v.tensor_scalar(rcnt[:, :], cnt[:, :], 1.0, None, ALU.max))
            link(v.reciprocal(rcnt[:, :], rcnt[:, :]))
            link(v.tensor_scalar(dinv2[:, :], cnt[:, :], 1.0, 1.0, ALU.add, ALU.max))
            edge_pass("gin2")
            node_phase("gin2")
            link(v.tensor_tensor(yn, yn, xn[:, :, :], ALU.add))
            layer_norm()
            ask_act(v.tensor_copy(dinv2[:, :], dinv2[:, :]))
            link(v.reciprocal(dinv[:, :], stat[:, :]))
            link(v.tensor_tensor(dinv2[:, :], dinv[:, :], dinv[:, :], ALU.mult))

            link(v.tensor_scalar(tb, xn[:, :, :], 0.0, None, ALU.max))
            link(v.tensor_tensor(tb, tb, over_features(dinv[:, :]), ALU.mult))
            table()
            turn("gin2")
            edge_pass("gcn1")
            node_phase("gcn1")
            table()
            turn("gcn1")
            edge_pass("gcn2")
            node_phase("gcn2")
            link(v.tensor_tensor(yn, yn, xn[:, :, :], ALU.add))
            layer_norm()

            link(v.tensor_copy(xc[:, :, :], xn[:, :, :]))
            for l, p in enumerate(SPLINE):
                table()
                link(v.memset(acc[0:C, :], 0.0))
                turn(p)
                edge_pass(p)
                node_phase(p)
                link(v.tensor_tensor(yn, yn, rn, ALU.add))
                if l < 2:
                    link(v.scalar_tensor_tensor(yn, yn, 0.01, yn, ALU.mult, ALU.max))
                link(v.tensor_tensor(yn, yn, xc[:, :, :], ALU.add))
                batch_norm(l)
            link(v.tensor_tensor(yn, xn[:, :, :], xc[:, :, :], ALU.add))
            layer_norm()

            link(v.tensor_copy(tb_att[:, :, 0:C], xn[:, :, :]))
            turn("collect")
            table()
            for h in range(2):
                dve.wait_ge(rows_out[h], 16 * TURNS)
            dve.wait_ge(scal_copied.sem, scal_copied.done("collect", halves - 1))
            chunk_turns("rows", SCAL)
            attention()
            chunk_turns("tiles", HEADS)
            table()
            link(v.memset(acc[:, :], 0.0))
            edge_pass("apply")
            node_phase("apply")
            link(v.tensor_tensor(yn, yn, xn[:, :, :], ALU.add))
            layer_norm()
            table()


def kernel(x, src, dst, edge_attr_3, L0_gnn_W1, L0_gnn_b1, L0_gnn_W2, L0_gnn_b2, L0_gnn_W3, L0_gnn_b3, L0_gnn_W4,
           L0_gnn_b4, L2_gnn_W1, L2_gnn_R1, L2_gnn_b1, L2_gnn_g1, L2_gnn_be1, L2_gnn_W2, L2_gnn_R2, L2_gnn_b2,
           L2_gnn_g2, L2_gnn_be2, L2_gnn_W3, L2_gnn_R3, L2_gnn_b3, L2_gnn_g3, L2_gnn_be3, L3_gnn_w, L3_gnn_fc_w,
           L3_gnn_fc_b, L3_gnn_bias):
    import numpy as np
    import concourse.bacc as bacc
    from concourse.bass_utils import run_bass_kernel_spmd

    x, src, dst, attr = (np.asarray(a) for a in (x, src, dst, edge_attr_3))
    x_pad = np.concatenate([x, np.zeros((NP - N, C), x.dtype)])
    pad = np.full(P * ET - E, N, src.dtype)
    src_pad, dst_pad = np.concatenate([src, pad]), np.concatenate([dst, pad])
    attr_pad = np.concatenate([attr, np.zeros((P * ET - E, 3), attr.dtype)])
    outside = np.full(1, -1, dst.dtype)
    arrays = {
        "x": x_pad,
        "src_tile": src_pad.reshape(ET, P).T,
        "dst_tile": dst_pad.reshape(ET, P).T,
        "dst_base": dst_pad.reshape(ET, P)[:, 0].reshape(1, ET),
        "src_row": src_pad.reshape(P, ET),
        "dst_ext": np.concatenate([outside, dst_pad, outside]),
        "attr_tile": attr_pad.reshape(ET, P, 3).transpose(1, 0, 2).reshape(P, ET * 3),
        "gW1": L0_gnn_W1, "gb1": L0_gnn_b1, "gW2": L0_gnn_W2, "gb2": L0_gnn_b2,
        "gW3": L0_gnn_W3, "gb3": L0_gnn_b3, "gW4": L0_gnn_W4, "gb4": L0_gnn_b4,
        "sW1": L2_gnn_W1, "sW2": L2_gnn_W2, "sW3": L2_gnn_W3, "sR1": L2_gnn_R1, "sR2": L2_gnn_R2, "sR3": L2_gnn_R3,
        "sb1": L2_gnn_b1, "sb2": L2_gnn_b2, "sb3": L2_gnn_b3, "sg1": L2_gnn_g1, "sg2": L2_gnn_g2, "sg3": L2_gnn_g3,
        "sbe1": L2_gnn_be1, "sbe2": L2_gnn_be2, "sbe3": L2_gnn_be3,
        "aw": L3_gnn_w, "fc_w": L3_gnn_fc_w, "fc_b": L3_gnn_fc_b, "abias": L3_gnn_bias,
    }
    arrays = {f"in_{k}": np.ascontiguousarray(v) for k, v in arrays.items()}
    nc = bacc.Bacc("TRN2", target_bir_lowering=False, num_devices=1)
    ap = {k[3:]: nc.dram_tensor(k, a.shape, mybir.dt.from_np(a.dtype), kind="ExternalInput").ap() for k, a in arrays.items()}
    out = nc.dram_tensor("out", (N, C), F32, kind="ExternalOutput").ap()

    def three(name):
        return [ap.pop(f"{name}{l}") for l in (1, 2, 3)]

    spline = {"sW": three("sW"), "sR": three("sR"), "sb_": three("sb"), "sg": three("sg"), "sbe": three("sbe")}
    build(nc, **ap, **spline, out=out)
    r = run_bass_kernel_spmd(nc, [arrays], core_ids=[0])
    return r.results[0]["out"]
```

```python
from contextlib import ExitStack

import concourse.bass as bass
from concourse import mybir

F32 = mybir.dt.float32
I32 = mybir.dt.int32
ALU = mybir.AluOpType
ACT = mybir.ActivationFunctionType
AX = mybir.AxisListType

P = 128
N = 12500
C = 32
HID = 64
NT = -(-N // P)
NP = NT * P
LAST_ROWS = N - (NT - 1) * P
E = 212500
G = 16
TW = 16
GW = 144
SUB = 4
SUBS = G // SUB
ET = 1664
TURNS = ET // (2 * G)
WIN = P
BT = 7
BN = BT * P
QT = P // C
QUADS = (0, BT - QT)
BLOCKS = NT // BT
RCH = ET // P
KS = 4
K12 = KS * KS
BASIS = KS + K12
HEADS = 4
SCAL = 2 * HEADS
L3ROW = C + SCAL
BIG = 1.0e30
EPS = 1e-5
assert ET * P >= E and NT % BT == 0 and BLOCKS % 2 == 0 and ET % P == 0


class Signal:

    def __init__(self, sem, plan, lead=0):
        self.sem, self.lead, self.plan, self.base, n = sem, lead, plan, {}, 0
        for phase, events in plan.items():
            self.base[phase] = n
            n += events

    def events(self, phase):
        return self.plan[phase]

    def done(self, phase, k):
        return k + (self.base[phase] + self.lead + 1)


def build(nc, x, src_tile, dst_tile, dst_base, half_base, src_row, dst_ext, attr_tile, gW1, gb1, gW2, gb2, gW3, gb3,
          gW4, gb4, sW, sR, sb_, sg, sbe, aw, fc_w, fc_b, abias, out):
    ctx = ExitStack()
    with ctx:
        def sb(name, shape, dt=F32):
            return ctx.enter_context(nc.sbuf_tensor(name, shape, dt))

        def sem(name):
            return ctx.enter_context(nc.semaphore(name))

        tab_h = nc.dram_tensor("tab_h", [NP, HID], F32).ap()
        tabs = {n: nc.dram_tensor(f"tab_{n}", [NP, C], F32).ap() for n in ("gcn1", "gcn2", "sp1", "sp2", "sp3")}
        tab_att = nc.dram_tensor("tab_att", [NP, L3ROW], F32).ap()
        basis_d = nc.dram_tensor("basis_d", [P, ET * BASIS], F32).ap()
        cnt_d = nc.dram_tensor("cnt_d", [NP], F32).ap()
        edge_rows = nc.dram_tensor("edge_rows", [P, ET * L3ROW], F32).ap()
        TABLE = {"gin1": x, "gin2": tab_h, "gcn1": tabs["gcn1"], "gcn2": tabs["gcn2"], "sp1": tabs["sp1"],
                 "sp2": tabs["sp2"], "sp3": tabs["sp3"], "collect": tab_att}
        ROW = {p: C for p in TABLE}
        ROW["gin2"], ROW["collect"] = HID, L3ROW
        PASSES = ["gin1", "gin2", "gcn1", "gcn2", "sp1", "sp2", "sp3", "collect", "apply"]
        SPLINE = ["sp1", "sp2", "sp3"]

        big = sb("big", [P, SCAL * ET])
        acc = big[:, 0:NP + WIN]
        rowch = big[:, :].rearrange("p (c e) -> p c e", c=SCAL)
        nodes = sb("nodes", [P, SCAL * ET])
        yn = nodes[:, 0:NT * C].rearrange("p (t c) -> p t c", c=C)
        rn = nodes[:, NT * C:2 * NT * C].rearrange("p (t c) -> p t c", c=C)
        tb_at = 2 * NT * C
        tb_h = nodes[:, tb_at:tb_at + NT * HID].rearrange("p (t c) -> p t c", c=HID)
        tb = nodes[:, tb_at:tb_at + NT * C].rearrange("p (t c) -> p t c", c=C)
        tb_att = nodes[:, tb_at:tb_at + NT * L3ROW].rearrange("p (t c) -> p t c", c=L3ROW)
        tilech = nodes[:, :].rearrange("p (c t) -> p c t", c=SCAL)
        xn = sb("xn", [P, NT, C])
        xc_flat = sb("xc", [P, NT * C])
        xc = xc_flat[:, :].rearrange("p (t c) -> p t c", c=C)
        loc = sb("loc", [P, ET])
        firsts_of = sb("firsts_of", [33, ET], I32)
        base = firsts_of[0:1, :]
        offs = firsts_of[32:33, :]
        work = sb("work", [P, 11136])
        at = [0]

        def carve(words):
            at[0] += words
            assert at[0] <= 11136
            return work[:, at[0] - words:at[0]]

        gbuf = carve(2 * G * HID).rearrange("p (h n) -> p h n", h=2)
        bs = carve(2 * G * BASIS).rearrange("p (h t k) -> p h t k", h=2, k=BASIS)
        u0 = carve(2 * SUB * P).rearrange("p (s t n) -> p s t n", s=2, n=P)
        fork = at[0]
        oh = carve(2 * G * WIN).rearrange("p (h t j) -> p h t j", h=2, j=WIN)
        ut = carve(2 * SUB * P).rearrange("p (s t n) -> p s t n", s=2, n=P)
        zb = carve(2 * 2 * K12 * C).rearrange("p (s t k c) -> p s t k c", s=2, t=2, c=C)
        msg = carve(2 * SUB * C).rearrange("p (s t c) -> p s t c", s=2, c=C)
        at[0] = fork
        mom = carve(2 * K12 * (GW + TW)).rearrange("p (h k n) -> p h k n", h=2, k=K12)
        vb = carve(SUB * K12 * TW).rearrange("p (s k j) -> p s k j", s=SUB, k=K12)
        oh_close = carve(2 * G * TW).rearrange("p (h t j) -> p h t j", h=2, j=TW)
        at[0] = fork
        oh_half = carve(2 * G * GW).rearrange("p (h t j) -> p h t j", h=2, j=GW)
        uh = carve(SUBS * SUB * P).rearrange("p (s t n) -> p s t n", s=SUBS, n=P)
        at[0] = 0
        stg = carve(2 * BN).rearrange("p (h n) -> p h n", h=2)
        hid = carve(2 * BN).rearrange("p (h n) -> p h n", h=2)
        xt = carve(2 * BN).rearrange("p (h n) -> p h n", h=2)
        stn = carve(2 * BT * C).rearrange("p (h t c) -> p h t c", h=2, c=C)
        sq = carve(NT * C).rearrange("p (t c) -> p t c", c=C)
        at[0] = 0
        cst = [carve(ET) for _ in range(2)]
        cont = cst[0]
        t1, pen_f, pen_b, pen_self = (carve(ET) for _ in range(4))
        target, first_target = pen_b, pen_self
        whf = carve(HEADS * C).rearrange("p (h c) -> p h c", c=C)
        fcr = carve(2 * C).rearrange("p (s c) -> p s c", c=C)
        vtmp = carve(SCAL * C).rearrange("p (s c) -> p s c", c=C)
        zero = sb("zero", [P, 1])
        half_prev = sb("half_prev", [1, 2 * TURNS + 1], I32)
        far = sb("far", [P, 1])
        far_i = sb("far_i", [1, 1], I32)
        attr = sb("attr", [P, 2, G, 3])
        hat = sb("hat", [P, G, 3, KS])
        bas = sb("bas", [P, 2, G, BASIS])

        ident = sb("ident", [P, P])
        ones = sb("ones", [P, P])
        iota_i = sb("iota_i", [P, GW], I32)
        iota_f = sb("iota_f", [P, GW])
        real = sb("real", [P, 1])
        epsc = sb("epsc", [P, 1])
        cnt = sb("cnt", [P, NT])
        cnt_rows = sb("cnt_rows", [NT, P])
        dinv = sb("dinv", [P, NT])
        dinv2 = sb("dinv2", [P, NT])
        rcnt = sb("rcnt", [P, NT])
        stat = sb("stat", [P, NT])
        stat2 = sb("stat2", [P, NT])
        colsum = sb("colsum", [P, C])
        mean = sb("mean", [P, C])
        rstd = sb("rstd", [P, C])
        w1 = sb("w1", [C, HID])
        w2 = sb("w2", [HID, HID])
        w3 = sb("w3", [HID, HID])
        w4 = sb("w4", [HID, C])
        b1c = sb("b1c", [HID, 1])
        b2c = sb("b2c", [HID, 1])
        b3c = sb("b3c", [HID, 1])
        b2r = sb("b2r", [P, HID])
        b4r = sb("b4r", [P, C])
        wk = sb("wk", [P, 3, K12, C])
        rw = sb("rw", [P, 3, P])
        sbr = sb("sbr", [P, 3, C])
        sgr = sb("sgr", [P, 3, C])
        sber = sb("sber", [P, 3, C])
        wh = sb("wh", [P, C])
        fcb = sb("fcb", [P, 1])
        v8r = sb("v8r", [P, SCAL])
        warm = sb("warm", [P, 1])
        v8 = sb("v8", [P, QT * SCAL])
        abr = sb("abr", [P, C])
        idx = sb("idx", [P, 2, G], I32)
        car = sb("car", [P, SCAL])
        pen8 = sb("pen8", [P, SCAL])
        carr = sb("carr", [SCAL, P])
        penr = sb("penr", [SCAL, P])
        carry = sb("carry", [SCAL, P + 1])
        init = sb("init", [P, SCAL])

        ps = ctx.enter_context(nc.psum_tensor("ps", [P, 8, 512], F32))

        halves, subs = 2 * TURNS, 2 * TURNS * SUBS
        every = {p: subs for p in PASSES if p != "collect"}
        made_u = {p: subs for p in SPLINE + ["apply"]}
        onehot_ready = Signal(sem("onehot_ready"), {p: halves for p in PASSES if p != "collect"})
        sums_ready = Signal(sem("sums_ready"), every, lead=2 * SUBS)
        added = Signal(sem("added"), {p: ET for p in PASSES if p != "collect"}, lead=2 * SUB)
        u_ready = Signal(sem("u_ready"), made_u, lead=2 * SUBS)
        ut_ps = Signal(sem("ut_ps"), {p: subs for p in SPLINE}, lead=2)
        ut_ready = Signal(sem("ut_ready"), {p: subs for p in SPLINE}, lead=2)
        z_ready = Signal(sem("z_ready"), {p: 2 * subs for p in SPLINE}, lead=4)
        y_ready = Signal(sem("y_ready"), {p: 2 * subs for p in SPLINE}, lead=4 * SUBS)
        msg_ready = Signal(sem("msg_ready"), {p: 2 * subs for p in SPLINE})
        v_ready = Signal(sem("v_ready"), {p: ET for p in SPLINE}, lead=2 * G)
        mom_ps = Signal(sem("mom_ps"), {p: ET for p in SPLINE}, lead=8)
        mom_added = Signal(sem("mom_added"), {p: ET for p in SPLINE}, lead=8)
        mom_zero = Signal(sem("mom_zero"), {p: halves + 2 for p in SPLINE})
        agg_ps = Signal(sem("agg_ps"), {p: halves + 1 for p in SPLINE}, lead=2)
        agg_added = Signal(sem("agg_added"), {**{p: halves + 1 for p in SPLINE}, "apply": halves}, lead=2)
        ONLY = {p: {"pe": ([mom_ps, agg_ps], [sums_ready, ut_ps, z_ready]),
                    "dve": ([v_ready, mom_added, agg_added], [onehot_ready, added, y_ready, msg_ready]),
                    "act": ([mom_zero], [ut_ready])} for p in SPLINE}
        ONLY["apply"] = {"dve": ([agg_added], [added])}
        far_known = sem("far_known")
        close_made = sem("close_made")
        near_in = sem("near_in")
        near_made = sem("near_made")
        scal_copied = Signal(sem("scal_copied"), {"collect": halves}, lead=2)
        idx_in = [sem("idx_in0"), sem("idx_in1")]
        basis_in = [sem("basis_in0"), sem("basis_in1")]
        gathered = {p: [sem(f"got_{p}{h}") for h in range(2)] for p in TABLE}
        rows_in = [sem("rows_in0"), sem("rows_in1")]
        rows_out = [sem("rows_out0"), sem("rows_out1")]
        attr_in = [sem("attr_in0"), sem("attr_in1")]
        bas_ready = Signal(sem("bas_ready"), {"gin1": halves}, lead=2)
        turn_chain = sem("turn_chain")
        bas_out = [sem("bas_out0"), sem("bas_out1")]
        held = {k: sem(f"held_{k}") for k in ("pool", "act", "dve", "pe")}
        consts = sem("consts")
        loads = sem("loads")
        rw_clear = sem("rw_clear")
        xload = sem("xload")
        chain = sem("chain")
        table_ready = sem("table_ready")
        ones_set = sem("ones_set")
        counted = sem("counted")
        cnt_out = sem("cnt_out")
        cnt_in = sem("cnt_in")
        seg_in = sem("seg_in")
        stored = sem("stored")
        out_stored = sem("out_stored")

        NODE = ["gin1", "gin2", "gcn1", "gcn2", "sp1", "sp2", "sp3", "apply"]
        HIDDEN = ["gin1", "gin2"]
        staged = Signal(sem("staged"), {p: BLOCKS for p in NODE})
        hid_ps = Signal(sem("hid_ps"), {p: BLOCKS for p in HIDDEN})
        hid_ready = Signal(sem("hid_ready"), {p: BLOCKS for p in HIDDEN}, lead=1)
        out_ps = Signal(sem("out_ps"), {p: BLOCKS for p in NODE}, lead=2)
        out_done = Signal(sem("out_done"), {p: BLOCKS for p in NODE}, lead=2)
        fm_done = Signal(sem("fm_done"), {"gin1": BLOCKS}, lead=1)
        TURNED = ["x", "gin2", "gcn1", "sp1", "sp2", "sp3", "collect"]
        PROJ = ["sp1", "sp2", "sp3", "collect"]
        tstaged = Signal(sem("tstaged"), {p: BLOCKS for p in TURNED})
        turned_ps = Signal(sem("turned_ps"), {p: BLOCKS for p in TURNED}, lead=2)
        turned = Signal(sem("turned"), {p: BLOCKS for p in TURNED}, lead=2)
        proj_ps = Signal(sem("proj_ps"), {p: BLOCKS for p in PROJ}, lead=2)
        proj_done = Signal(sem("proj_done"), {p: BLOCKS for p in PROJ}, lead=2)
        to_pe = sem("to_pe")
        from_pe = sem("from_pe")
        to_act = sem("to_act")
        from_act = sem("from_act")
        cstaged = Signal(sem("cstaged"), {"rows": SCAL, "tiles": HEADS})
        cturn_ps = Signal(sem("cturn_ps"), {"rows": SCAL, "tiles": HEADS}, lead=2)
        cturned = Signal(sem("cturned"), {"rows": SCAL, "tiles": HEADS}, lead=1)

        LEADS = {"pe": [sums_ready, ut_ps, z_ready, mom_ps, agg_ps, out_ps, turned_ps, proj_ps, cturn_ps],
                 "dve": [added, u_ready, y_ready, v_ready, mom_added, agg_added, bas_ready, out_done, proj_done],
                 "act": [ut_ready, hid_ready, fm_done, turned, cturned, scal_copied]}

        def lead_in(eng, name):
            for s in LEADS[name]:
                eng.sem_inc(s.sem, s.lead)

        def two_ways(eng, name, p, close, wide):
            eng.wait_ge(far_known, 1)
            is_far = eng.value_load(far_i[0:1, 0:1], min_val=0, max_val=1)
            of_close, of_wide = ONLY[p].get(name, ([], []))
            with eng.If(is_far == 0):
                close(p)
                for s in of_wide:
                    eng.sem_inc(s.sem, s.events(p))
            with eng.Else():
                wide(p)
                for s in of_close:
                    eng.sem_inc(s.sem, s.events(p))

        def hold(eng, name, s, value):
            eng.wait_ge(s, value)
            eng.sem_inc(held[name], 1)


        def rows(p, h):
            w = {"gin1": C + 4, "apply": L3ROW}.get(p) or ROW[p]
            return gbuf[:, h, 0:G * w].rearrange("p (t c) -> p t c", c=w)

        def acc_rows(p):
            return {"gin1": C + 1, "gin2": HID, "apply": P}.get(p, C)

        def flat(bank, n, rows_=P):
            return ps[0:rows_, bank:bank + -(-n // 512), :].rearrange("p b n -> p (b n)")[:, 0:n]

        STORES = ["gin2", "gcn1", "gcn2", "sp1", "sp2", "sp3", "collect"]
        LOADS = [
            (w1[:, :], gW1), (w2[:, :], gW2), (w3[:, :], gW3), (w4[:, :], gW4),
            (b1c[:, :], gb1.unsqueeze(1)), (b2c[:, :], gb2.unsqueeze(1)), (b3c[:, :], gb3.unsqueeze(1)),
            (b2r[:, :], gb2.partition_broadcast(P)), (b4r[:, :], gb4.partition_broadcast(P)),
            (wh[:, :], aw.rearrange("h f o -> (h f) o")),
            (fcr[:, :, :].rearrange("p s o -> p (s o)"), fc_w.broadcast_to([P, 2 * C])),
            (fcb[:, :], fc_b.partition_broadcast(P)), (abr[:, :], abias.partition_broadcast(P)),
        ]
        for q in range(QT):
            LOADS.append((whf[q * C:(q + 1) * C, :, :], aw.rearrange("h f o -> f h o")))
        for l in range(3):
            for k0 in range(KS):
                LOADS.append((wk[k0 * C:(k0 + 1) * C, l, :, :], sW[l].rearrange("(k m) c o -> m c k o", m=KS)[k0]))
            for q in range(QT):
                LOADS.append((rw[q * C:(q + 1) * C, l, q * C:(q + 1) * C], sR[l]))
            for dst, v in ((sbr, sb_), (sgr, sg), (sber, sbe)):
                LOADS.append((dst[:, l, :], v[l].partition_broadcast(P)))

        block = ctx.enter_context(nc.Block())

        @block.sync
        def _(sp):
            sp.dma_start(xn[:, :, :], x.rearrange("(t p) c -> p t c", p=P)).then_inc(xload, 16)
            for dst, src in ((target.bitcast(I32), dst_tile), (first_target.bitcast(I32), dst_base.broadcast_to([P, ET])),
                             (base[:, :], dst_base)):
                sp.dma_start(dst, src).then_inc(xload, 16)

            def store_table(p):
                n = STORES.index(p) + 1
                src = {"gin2": tb_h, "gcn1": tb, "gcn2": tb, "collect": tb_att}.get(p, xc[:, :, :])
                sp.wait_ge(table_ready, n)
                sp.dma_start(TABLE[p].rearrange("(t p) c -> p t c", p=P), src).then_inc(stored, 16)

            def index_loads(p, close=False):
                with sp.Fori(0, TURNS) as i:
                    for h in range(2):
                        k, tile0 = 2 * i + h, (2 * i + h) * G
                        if p != "apply":
                            sp.wait_ge(gathered[p][h], i * (16 * G))
                            sp.dma_start(idx[:, h, :], src_tile[:, bass.ds(tile0, G)]).then_inc(idx_in[h], 16)
                        if p == "gin1":
                            sp.wait_ge(bas_ready.sem, bas_ready.done(p, k - 2))
                            sp.dma_start(attr[:, h, :, :].rearrange("p t d -> p (t d)"),
                                         attr_tile[:, bass.ds(tile0 * 3, G * 3)]).then_inc(attr_in[h], 16)
                        if p in SPLINE:
                            if close:
                                sp.wait_ge(v_ready.sem, v_ready.done(p, G * (k - 2) + G - 1))
                            else:
                                sp.wait_ge(y_ready.sem, y_ready.done(p, 2 * SUBS * (k - 2) + 2 * SUBS - 1))
                            sp.dma_start(bs[:, h, :, :].rearrange("p t k -> p (t k)"),
                                         basis_d[:, bass.ds(tile0 * BASIS, G * BASIS)]).then_inc(basis_in[h], 16)
                        if p == "apply":
                            sp.wait_ge(u_ready.sem, u_ready.done(p, SUBS * (k - 2) + SUBS - 1))
                            sp.dma_start(gbuf[:, h, 0:G * L3ROW],
                                         edge_rows[:, bass.ds(tile0 * L3ROW, G * L3ROW)]).then_inc(rows_in[h], 16)

            index_loads("gin1")
            sp.wait_ge(counted, 1)
            sp.dma_start(cnt_d.unsqueeze(0), acc[C:C + 1, 0:NP]).then_inc(cnt_out, 16)
            sp.wait_ge(cnt_out, 16)
            sp.dma_start(cnt_rows[:, :], cnt_d.rearrange("(t p) -> t p", p=P)).then_inc(cnt_in, 16)
            for p in PASSES[1:-1]:
                store_table(p)
                if p == "sp1":
                    for h in range(2):
                        sp.wait_ge(bas_out[h], 16 * TURNS)
                if p in SPLINE:
                    two_ways(sp, "sp", p, lambda p: index_loads(p, close=True), index_loads)
                elif p == "collect":
                    for dst, src in ((t1, dst_ext[1:1 + P * ET]), (pen_f, dst_ext[0:P * ET]),
                                     (pen_b, dst_ext[2:2 + P * ET])):
                        sp.dma_start(dst.bitcast(I32), src.rearrange("(p e) -> p e", p=P)).then_inc(seg_in, 16)
                    sp.dma_start(pen_self.bitcast(I32), src_row).then_inc(seg_in, 16)
                    index_loads(p)
                else:
                    index_loads(p)
            sp.wait_ge(scal_copied.sem, scal_copied.done("collect", halves - 1))
            sp.dma_start(xc_flat[:, 0:ET].bitcast(I32), dst_tile).then_inc(near_in, 16)
            sp.dma_start(xc_flat[:, ET:ET + 2 * TURNS].bitcast(I32),
                         half_base.broadcast_to([P, 2 * TURNS])).then_inc(near_in, 16)
            for h in range(2):
                sp.wait_ge(rows_out[h], 16 * TURNS)
            sp.wait_ge(table_ready, len(STORES) + 1)
            index_loads("apply")
            sp.wait_ge(table_ready, len(STORES) + 2)
            full = NT - 1
            sp.dma_start(out[0:full * P, :].rearrange("(t p) c -> p t c", p=P), xn[:, 0:full, :]).then_inc(out_stored, 16)
            sp.dma_start(out[full * P:N, :], xn[0:LAST_ROWS, full, :]).then_inc(out_stored, 16)
            sp.wait_ge(out_stored, 32)

        @block.gpsimd
        def _(pool):
            pool.memset(rw[:, :, :], 0.0).then_inc(rw_clear, 1)
            pool.memset(ones[:, :], 1.0).then_inc(consts, 1)
            pool.memset(ident[:, :], 0.0).then_inc(consts, 1)
            pool.memset(real[:, :], 1.0).then_inc(consts, 1)
            pool.iota(iota_i[:, :], pattern=[[1, GW]], base=0, channel_multiplier=0).then_inc(consts, 1)
            pool.wait_ge(consts, 4)
            pool.affine_select(out=ident[:, :], in_=ident[:, :], compare_op=ALU.not_equal, fill=1.0, base=0,
                               pattern=[[-1, P]], channel_multiplier=1).then_inc(consts, 1)
            pool.affine_select(out=real[:, :], in_=real[:, :], compare_op=ALU.is_ge, fill=0.0,
                               base=LAST_ROWS - 1, pattern=[[0, 1]], channel_multiplier=-1).then_inc(consts, 1)

            def gathers(p):
                if p != "gin1":
                    hold(pool, "pool", stored, 16 * (STORES.index(p) + 1))
                else:
                    hold(pool, "pool", ones_set, 1)
                with pool.Fori(0, TURNS) as i:
                    for h in range(2):
                        k = 2 * i + h
                        if p in SPLINE:
                            hold(pool, "pool", u_ready.sem, u_ready.done(p, SUBS * (k - 2) + SUBS - 1))
                        elif p == "collect":
                            hold(pool, "pool", scal_copied.sem, scal_copied.done(p, k - 2))
                            hold(pool, "pool", rows_out[h], 16 * i)
                        else:
                            hold(pool, "pool", sums_ready.sem, sums_ready.done(p, SUBS * (k - 2) + SUBS - 1))
                        hold(pool, "pool", idx_in[h], (i + 1) * 16 + 16 * TURNS * PASSES.index(p))
                        for t in range(G):
                            pool.indirect_dma_start(
                                out=rows(p, h)[:, t, 0:ROW[p]], out_offset=None, in_=TABLE[p],
                                in_offset=bass.IndirectOffsetOnAxis(ap=idx[:, h, t:t + 1], axis=0),
                            ).then_inc(gathered[p][h], 16)

            def weigh_rows(p):
                with pool.Fori(0, TURNS) as i:
                    for h in range(2):
                        k = 2 * i + h
                        hold(pool, "pool", rows_in[h], (i + 1) * 16)
                        for s in range(SUBS):
                            hold(pool, "pool", sums_ready.sem, sums_ready.done(p, SUBS * (k - 1) + s))
                            pool.tensor_tensor(
                                uh[:, s, :, :].rearrange("p t (a c) -> p t a c", c=C),
                                rows(p, h)[:, s * SUB:(s + 1) * SUB, 0:C].unsqueeze(2).broadcast_to([P, SUB, HEADS, C]),
                                tilech[:, 0:HEADS, bass.ds(k * G + s * SUB, SUB)].rearrange("p h t -> p t h")
                                .unsqueeze(3).broadcast_to([P, SUB, HEADS, C]), ALU.mult).then_inc(u_ready.sem, 1)

            for p in PASSES[:-1]:
                gathers(p)
            pool.wait_ge(table_ready, len(STORES) + 1)
            two_ways(pool, "pool", "apply", weigh_rows, lambda p: None)

        @block.tensor
        def _(pe):
            lead_in(pe, "pe")
            asked = [0]

            def answer(emit):
                asked[0] += 1
                pe.wait_ge(to_pe, asked[0])
                emit().then_inc(from_pe, 1)

            def window_sums(p, k, h, s, rhs_row):
                g = SUBS * k + s
                pe.wait_ge(added.sem, added.done(p, SUB * (g - 2) + SUB - 1))
                for q in range(SUB):
                    m = acc_rows(p)
                    last = nc.tensor.matmul(ps[0:m, 6 + s % 2, q * WIN:(q + 1) * WIN], rhs_row(q),
                                            oh[:, h, s * SUB + q, :], start=True, stop=True)
                last.then_inc(sums_ready.sem, 1)

            def turns_of_rows(p, k, s):
                g = SUBS * k + s
                hold(pe, "pe", u_ready.sem, u_ready.done(p, g))
                pe.wait_ge(ut_ready.sem, ut_ready.done(p, g - 2))
                for q in range(SUB):
                    last = nc.tensor.transpose(ps[:, s % 2, q * P:(q + 1) * P], u0[:, s % 2, q, :], ident[:, :])
                last.then_inc(ut_ps.sem, 1)

            def kernels_product(p, k, s, half):
                u = 2 * (SUBS * k + s) + half
                hold(pe, "pe", ut_ready.sem, ut_ready.done(p, SUBS * k + s))
                pe.wait_ge(y_ready.sem, y_ready.done(p, u - 2))
                for q in range(2):
                    last = nc.tensor.matmul(ps[:, 2 + 2 * half + q, :], ut[:, s % 2, 2 * half + q, :],
                                            wk[:, SPLINE.index(p), :, :].rearrange("p k c -> p (k c)"),
                                            start=True, stop=True)
                last.then_inc(z_ready.sem, 1)

            def message_sums(p, k, h, s):
                hold(pe, "pe", msg_ready.sem, msg_ready.done(p, 2 * (SUBS * k + s) + 1))
                window_sums(p, k, h, s, lambda q: msg[:, s % 2, q, :])

            def edge_pass(p):
                with pe.Fori(0, TURNS) as i:
                    for h in range(2):
                        k = 2 * i + h
                        hold(pe, "pe", onehot_ready.sem, onehot_ready.done(p, k))
                        if p in SPLINE:
                            turns_of_rows(p, k, 0)
                            turns_of_rows(p, k, 1)
                            for s in range(SUBS):
                                kernels_product(p, k, s, 0)
                                kernels_product(p, k, s, 1)
                                if s >= 1:
                                    message_sums(p, k, h, s - 1)
                                    if s + 1 < SUBS:
                                        turns_of_rows(p, k, s + 1)
                            message_sums(p, k, h, SUBS - 1)
                        elif p == "apply":
                            for s in range(SUBS):
                                hold(pe, "pe", u_ready.sem, u_ready.done(p, SUBS * k + s))
                                window_sums(p, k, h, s, lambda q: u0[:, s % 2, q, :])
                        else:
                            hold(pe, "pe", gathered[p][h], (i + 1) * (16 * G))
                            for s in range(SUBS):
                                window_sums(p, k, h, s, lambda q: rows(p, h)[:, s * SUB + q, 0:acc_rows(p)])

            def moments(p):
                l = SPLINE.index(p)

                def times_kernels(k, h, part):
                    if part == 0:
                        hold(pe, "pe", mom_added.sem, mom_added.done(p, G * k - 1))
                        hold(pe, "pe", mom_zero.sem, mom_zero.done(p, k))
                        hold(pe, "pe", agg_added.sem, agg_added.done(p, k - 2))
                    for kk in range(part * SUBS, (part + 1) * SUBS):
                        last = nc.tensor.matmul(ps[0:C, 4 + h, 0:GW], wk[:, l, kk, :], mom[:, 1 - h, kk, 0:GW],
                                                start=(kk == 0), stop=(kk == K12 - 1))
                    if part == K12 // SUBS - 1:
                        last.then_inc(agg_ps.sem, 1)

                with pe.Fori(0, TURNS) as i:
                    for h in range(2):
                        k = 2 * i + h
                        for t in range(G):
                            n, s = G * k + t, t // SUB
                            if t % SUB == 0:
                                hold(pe, "pe", u_ready.sem, u_ready.done(p, SUBS * k + s))
                            hold(pe, "pe", v_ready.sem, v_ready.done(p, n))
                            pe.wait_ge(mom_added.sem, mom_added.done(p, n - SUB))
                            nc.tensor.matmul(ps[:, t % SUB, 0:K12 * TW], u0[:, s % 2, t % SUB, :],
                                             vb[:, t % SUB, :, :].rearrange("p k j -> p (k j)"),
                                             start=True, stop=True).then_inc(mom_ps.sem, 1)
                            if t >= SUB and t % 2 == 1 and (t - SUB) // 2 < SUBS:
                                times_kernels(k, h, (t - SUB) // 2)
                for part in range(SUBS):
                    times_kernels(2 * TURNS, 0, part)

            def half_sums(p):
                with pe.Fori(0, TURNS) as i:
                    for h in range(2):
                        k = 2 * i + h
                        hold(pe, "pe", onehot_ready.sem, onehot_ready.done(p, k))
                        hold(pe, "pe", agg_added.sem, agg_added.done(p, k - 2))
                        for t in range(G):
                            s = t // SUB
                            if t % SUB == 0:
                                hold(pe, "pe", u_ready.sem, u_ready.done(p, SUBS * k + s))
                            last = nc.tensor.matmul(ps[:, 4 + h, 0:GW], uh[:, s, t % SUB, :], oh_half[:, h, t, :],
                                                    start=(t == 0), stop=(t == G - 1))
                            if t % SUB == SUB - 1:
                                last.then_inc(sums_ready.sem, 1)

            def turn(name):
                proj = {"sp1": rw[:, 0, :], "sp2": rw[:, 1, :], "sp3": rw[:, 2, :], "collect": v8[:, :]}.get(name)
                with pe.Fori(0, BLOCKS // 2) as i:
                    for h in range(2):
                        b = 2 * i + h
                        hold(pe, "pe", tstaged.sem, tstaged.done(name, b))
                        pe.wait_ge(turned.sem, turned.done(name, b - 2))
                        if proj is None:
                            for j in range(BT):
                                last = nc.tensor.transpose(flat(2 * h, BN, C)[:, j * P:(j + 1) * P],
                                                           stn[:, h, j, :], ident[:, :])
                        else:
                            for q, j in enumerate(QUADS):
                                last = nc.tensor.transpose(ps[:, 2 * h, q * P:(q + 1) * P],
                                                           stn[:, h, j:j + QT, :].rearrange("p t c -> p (t c)"),
                                                           ident[:, :])
                        last.then_inc(turned_ps.sem, 1)
                    if proj is not None:
                        for h in range(2):
                            b, w = 2 * i + h, proj.shape[-1] // QT
                            hold(pe, "pe", turned.sem, turned.done(name, b))
                            pe.wait_ge(proj_done.sem, proj_done.done(name, b - 2))
                            for q, j in enumerate(QUADS):
                                last = nc.tensor.matmul(ps[:, 4 + h, j * w:(j + QT) * w],
                                                        xt[:, h, q * P:(q + 1) * P], proj, start=True, stop=True)
                            last.then_inc(proj_ps.sem, 1)

            def node_phase(p):
                first, bank = {"gin1": (w1, 0), "gin2": (w3, 0)}.get(p), None
                second = {"gin1": w2[:, :], "gin2": w4[:, :], "apply": wh[:, :]}.get(p)
                w = C if second is None else second.shape[-1]
                m = {"gin1": HID, "gin2": HID, "apply": P}.get(p, C)
                with pe.Fori(0, BLOCKS // 2) as i:
                    if first is not None:
                        for h in range(2):
                            b = 2 * i + h
                            hold(pe, "pe", staged.sem, staged.done(p, b))
                            hold(pe, "pe", hid_ready.sem, hid_ready.done(p, b - 1))
                            kk = C if p == "gin1" else HID
                            for c0, c1 in ((0, 512), (512, BN)):
                                last = nc.tensor.matmul(flat(0, BN, HID)[:, c0:c1], first[0][:, :],
                                                        stg[0:kk, h, c0:c1], start=True, stop=True)
                            last.then_inc(hid_ps.sem, 1)
                    for h in range(2):
                        b = 2 * i + h
                        if first is not None:
                            hold(pe, "pe", hid_ready.sem, hid_ready.done(p, b))
                        else:
                            hold(pe, "pe", staged.sem, staged.done(p, b))
                        src = hid if first is not None else stg
                        hold(pe, "pe", out_done.sem, out_done.done(p, b - 2))
                        if p == "gin1":
                            hold(pe, "pe", fm_done.sem, fm_done.done(p, b - 1))
                            for c0, c1 in ((0, 512), (512, BN)):
                                nc.tensor.matmul(flat(2, BN, HID)[:, c0:c1], w2[:, :], hid[0:HID, h, c0:c1],
                                                 start=True, stop=True)
                        for j in range(BT):
                            to, tile = ps[:, 4 + h, j * w:(j + 1) * w], src[0:m, h, j * P:(j + 1) * P]
                            if second is None:
                                last = nc.tensor.transpose(to, tile, ident[0:C, 0:C])
                            else:
                                last = nc.tensor.matmul(to, tile, second, start=True, stop=True)
                        last.then_inc(out_ps.sem, 1)

            def col_sums():
                answer(lambda: nc.tensor.matmul(ps[:, 7, 0:C], ones[:, :], colsum[:, :], start=True, stop=True))

            def chunk_turns(name, n):
                with pe.Fori(0, n // 2) as i:
                    for h in range(2):
                        c = 2 * i + h
                        hold(pe, "pe", cstaged.sem, cstaged.done(name, c))
                        pe.wait_ge(cturned.sem, cturned.done(name, c - 1))
                        for r in range(RCH):
                            last = nc.tensor.transpose(flat(0, ET)[:, r * P:(r + 1) * P],
                                                       cst[h][:, r * P:(r + 1) * P], ident[:, :])
                        last.then_inc(cturn_ps.sem, 1)

            pe.wait_ge(consts, 6)
            turn("x")
            answer(lambda: nc.tensor.transpose(ps[0:1, 7, 0:P], far[:, :], ident[:, :]))
            edge_pass("gin1")
            pe.wait_ge(loads, 16 * len(LOADS))
            node_phase("gin1")
            answer(lambda: nc.tensor.transpose(ps[:, 7, 0:NT], cnt_rows[:, :], ident[0:NT, 0:NT]))
            edge_pass("gin2")
            node_phase("gin2")
            turn("gin2")
            edge_pass("gcn1")
            node_phase("gcn1")
            turn("gcn1")
            edge_pass("gcn2")
            node_phase("gcn2")
            for p in SPLINE:
                turn(p)
                two_ways(pe, "pe", p, moments, edge_pass)
                node_phase(p)
                col_sums()
                col_sums()
            turn("collect")
            chunk_turns("rows", SCAL)
            for carry_in in (carry[:, 0:P], carry[:, 1:P + 1]) * 2:
                answer(lambda: nc.tensor.transpose(ps[0:SCAL, 5, 0:P], car[:, :], ident[:, :]))
                answer(lambda: nc.tensor.transpose(ps[0:SCAL, 5, P:2 * P], pen8[:, :], ident[:, :]))
                answer(lambda: nc.tensor.transpose(ps[:, 6, 0:SCAL], carry_in, ident[0:SCAL, 0:SCAL]))
            chunk_turns("tiles", HEADS)
            two_ways(pe, "pe", "apply", half_sums, edge_pass)
            node_phase("apply")

        @block.scalar
        def _(act):
            lead_in(act, "act")
            asked = [0]

            def answer(emit):
                asked[0] += 1
                act.wait_ge(to_act, asked[0])
                emit().then_inc(from_act, 1)

            def root(n):
                if n == C:
                    answer(lambda: nc.scalar.activation(stat2[:, :], stat[:, :], ACT.Sqrt, bias=epsc[:, :], scale=1.0 / C))
                else:
                    answer(lambda: nc.scalar.activation(mean[:, :], ps[:, 7, 0:C], ACT.Sqrt, bias=epsc[:, :], scale=1.0 / N))

            def turn(name):
                with act.Fori(0, BLOCKS // 2) as i:
                    for h in range(2):
                        b = 2 * i + h
                        hold(act, "act", turned_ps.sem, turned_ps.done(name, b))
                        if name in PROJ:
                            hold(act, "act", proj_ps.sem, proj_ps.done(name, b - 2))
                            dst, src = xt[:, h, 0:len(QUADS) * P], ps[:, 2 * h, 0:len(QUADS) * P]
                        else:
                            dst, src = acc[0:C, bass.ds(b * BN, BN)], flat(2 * h, BN, C)
                        nc.scalar.activation(dst, src, ACT.Copy).then_inc(turned.sem, 1)

            def hidden(p):
                bias = {"gin1": b1c, "gin2": b3c}[p]
                with act.Fori(0, BLOCKS // 2) as i:
                    for h in range(2):
                        b = 2 * i + h
                        hold(act, "act", hid_ps.sem, hid_ps.done(p, b))
                        hold(act, "act", out_ps.sem, out_ps.done(p, b - 2))
                        nc.scalar.activation(hid[0:HID, h, :], flat(0, BN, HID), ACT.Relu,
                                             bias=bias[:, :]).then_inc(hid_ready.sem, 1)
                    for h in range(2):
                        b = 2 * i + h
                        if p == "gin1":
                            hold(act, "act", cnt_out, 16)
                            hold(act, "act", out_ps.sem, out_ps.done(p, b))
                            nc.scalar.activation(acc[0:HID, bass.ds(b * BN, BN)], flat(2, BN, HID), ACT.Relu,
                                                 bias=b2c[:, :]).then_inc(fm_done.sem, 1)

            def store_basis():
                with act.Fori(0, TURNS) as i:
                    for h in range(2):
                        k = 2 * i + h
                        act.wait_ge(bas_ready.sem, bas_ready.done("gin1", k))
                        act.dma_start(basis_d[:, bass.ds(k * (G * BASIS), G * BASIS)],
                                      bas[:, h, :, :].rearrange("p t k -> p (t k)")).then_inc(bas_out[h], 16)

            def copy_turned_rows(p):
                with act.Fori(0, TURNS) as i:
                    for h in range(2):
                        for s in range(SUBS):
                            g = SUBS * (2 * i + h) + s
                            hold(act, "act", ut_ps.sem, ut_ps.done(p, g))
                            act.wait_ge(z_ready.sem, z_ready.done(p, 2 * (g - 2) + 1))
                            nc.scalar.activation(ut[:, s % 2, :, :].rearrange("p t n -> p (t n)"), ps[:, s % 2, :],
                                                 ACT.Copy).then_inc(ut_ready.sem, 1)

            def clear_moments(p):
                def clear(h):
                    return nc.scalar.activation(mom[:, h, :, :], zero[:, :].unsqueeze(2).broadcast_to([P, K12, GW + TW]), ACT.Copy)

                clear(1).then_inc(mom_zero.sem, 1)
                clear(0).then_inc(mom_zero.sem, 1)
                with act.Fori(0, TURNS) as i:
                    for h in range(2):
                        k = 2 * i + h
                        hold(act, "act", agg_ps.sem, agg_ps.done(p, k))
                        clear(1 - h).then_inc(mom_zero.sem, 1)

            def collect():
                with act.Fori(0, TURNS) as i:
                    for h in range(2):
                        k = 2 * i + h
                        hold(act, "act", gathered["collect"][h], (i + 1) * (16 * G))
                        act.dma_start(edge_rows[:, bass.ds(k * (G * L3ROW), G * L3ROW)],
                                      gbuf[:, h, 0:G * L3ROW]).then_inc(rows_out[h], 16)
                        nc.scalar.activation(tilech[:, :, bass.ds(k * G, G)],
                                             rows("collect", h)[:, :, C:L3ROW].rearrange("p t c -> p c t"),
                                             ACT.Copy).then_inc(scal_copied.sem, 1)

            def chunk_turns(name, n):
                with act.Fori(0, n // 2) as i:
                    for h in range(2):
                        c = 2 * i + h
                        hold(act, "act", cturn_ps.sem, cturn_ps.done(name, c))
                        src = flat(0, ET)
                        if name == "rows":
                            dst = big[:, bass.ds(c * ET, ET)]
                        else:
                            src = src.rearrange("p (r q) -> p r q", r=RCH)
                            dst = nodes[:, bass.ds(c * ET, ET)].rearrange("p (q r) -> p r q", r=RCH)
                        nc.scalar.activation(dst, src, ACT.Copy).then_inc(cturned.sem, 1)

            act.wait_ge(ones_set, 1)
            nc.scalar.activation(warm[:, :], gbuf[:, 0, C:C + 1], ACT.Copy)
            turn("x")
            act.wait_ge(rw_clear, 1)
            for dst, src in LOADS:
                act.dma_start(dst, src).then_inc(loads, 16)
            store_basis()
            act.wait_ge(loads, 16 * len(LOADS))
            hidden("gin1")
            hidden("gin2")
            root(C)
            answer(lambda: nc.scalar.activation(stat[:, :], dinv2[:, :], ACT.Sqrt))
            turn("gin2")
            turn("gcn1")
            root(C)
            for p in SPLINE:
                turn(p)
                hold(act, "act", proj_ps.sem, proj_ps.done(p, BLOCKS - 1))
                two_ways(act, "act", p, clear_moments, copy_turned_rows)
                root(N)
            root(C)
            turn("collect")
            collect()
            chunk_turns("rows", SCAL)
            heads = big[:, 0:HEADS * ET]
            answer(lambda: nc.scalar.activation(heads, heads, ACT.Exp))
            chunk_turns("tiles", HEADS)
            root(C)

        @block.vector
        def _(dve):
            lead_in(dve, "dve")
            count, turn_base, to_act_n, to_pe_n = [0], [0], [0], [0]
            regs = [dve.alloc_register(f"first{t}") for t in range(G)]
            v = nc.vector

            def link(ins):
                count[0] += 1
                ins.then_inc(chain, 1)
                dve.wait_ge(chain, count[0])

            class TurnLink:

                def __init__(self, i, n):
                    self.i, self.n, self.k = i, n, 0

                def __call__(self, ins):
                    self.k += 1
                    assert self.k <= self.n
                    ins.then_inc(turn_chain, 1)
                    dve.wait_ge(turn_chain, self.i * self.n + (turn_base[0] + self.k))

                def close(self, turns):
                    assert self.k == self.n
                    turn_base[0] += self.n * turns

            def ask_act(ins):
                to_act_n[0] += 1
                ins.then_inc(to_act, 1)
                dve.wait_ge(from_act, to_act_n[0])

            def ask_pe(ins):
                to_pe_n[0] += 1
                ins.then_inc(to_pe, 1)
                dve.wait_ge(from_pe, to_pe_n[0])

            def over_tiles(row):
                return row.unsqueeze(1).broadcast_to([P, NT, C])

            def over_features(col, n=NT):
                return col.unsqueeze(2).broadcast_to([P, n, C])

            def layer_norm():
                link(v.tensor_reduce(stat[:, :], yn, axis=AX.X, op=ALU.add))
                link(v.tensor_scalar(stat[:, :], stat[:, :], 1.0 / C, None, ALU.mult))
                link(v.tensor_tensor(yn, yn, over_features(stat[:, :]), ALU.subtract))
                link(v.tensor_tensor(sq, yn, yn, ALU.mult))
                ask_act(v.tensor_reduce(stat[:, :], sq, axis=AX.X, op=ALU.add))
                link(v.reciprocal(stat[:, :], stat2[:, :]))
                link(v.tensor_tensor(xn[:, :, :], yn, over_features(stat[:, :]), ALU.mult))

            def batch_norm(l):
                last, cols = NT - 1, (lambda a: a.rearrange("p t c -> p c t"))
                link(v.tensor_scalar(yn[:, last, :], yn[:, last, :], real[:, :], None, ALU.mult))
                ask_pe(v.tensor_reduce(colsum[:, :], cols(yn), axis=AX.X, op=ALU.add))
                link(v.tensor_scalar(mean[:, :], ps[:, 7, 0:C], 1.0 / N, None, ALU.mult))
                link(v.tensor_tensor(yn, yn, over_tiles(mean[:, :]), ALU.subtract))
                link(v.tensor_scalar(yn[:, last, :], yn[:, last, :], real[:, :], None, ALU.mult))
                link(v.tensor_tensor(sq, yn, yn, ALU.mult))
                ask_pe(v.tensor_reduce(colsum[:, :], cols(sq), axis=AX.X, op=ALU.add))
                ask_act(v.tensor_scalar(stat[:, 0:1], epsc[:, :], 1.0, None, ALU.mult))
                link(v.reciprocal(rstd[:, :], mean[:, :]))
                link(v.tensor_tensor(rstd[:, :], rstd[:, :], sgr[:, l, :], ALU.mult))
                link(v.tensor_tensor(yn, yn, over_tiles(rstd[:, :]), ALU.mult))
                link(v.tensor_tensor(xc[:, :, :], yn, over_tiles(sber[:, l, :]), ALU.add))

            def turn(name):
                src = {"x": xn[:, :, :], "gin2": tb, "gcn1": tb, "collect": xn[:, :, :]}.get(name, xc[:, :, :])
                with dve.Fori(0, BLOCKS // 2) as i:
                    for h in range(2):
                        b = 2 * i + h
                        hold(dve, "dve", turned_ps.sem, turned_ps.done(name, b - 2))
                        v.tensor_copy(stn[:, h, :, :], src[:, bass.ds(b * BT, BT), :]).then_inc(tstaged.sem, 1)
                    if name in PROJ:
                        for h in range(2):
                            b = 2 * i + h
                            dve.wait_ge(proj_ps.sem, proj_ps.done(name, b))
                            if name == "collect":
                                got = ps[:, 4 + h, 0:BT * SCAL].rearrange("p (t c) -> p t c", c=SCAL)
                                ins = v.tensor_scalar(tb_att[:, bass.ds(b * BT, BT), C:L3ROW], got, 1.0, None, ALU.mult)
                            else:
                                got = ps[:, 4 + h, 0:BT * C].rearrange("p (t c) -> p t c", c=C)
                                bias = sbr[:, SPLINE.index(name), :].unsqueeze(1).broadcast_to([P, BT, C])
                                ins = v.tensor_tensor(rn[:, bass.ds(b * BT, BT), :], got, bias, ALU.add)
                            ins.then_inc(proj_done.sem, 1)
                if name in PROJ:
                    dve.wait_ge(proj_done.sem, proj_done.done(name, BLOCKS - 1))
                else:
                    dve.wait_ge(turned.sem, turned.done(name, BLOCKS - 1))

            def node_phase(p):
                kk = acc_rows(p)
                dve.wait_ge(added.sem, added.done(p, ET - 1))
                if p in agg_added.plan:
                    dve.wait_ge(agg_added.sem, agg_added.done(p, agg_added.events(p) - 1))
                if p in SPLINE:
                    dve.wait_ge(mom_zero.sem, mom_zero.done(p, halves + 1))
                with dve.Fori(0, BLOCKS // 2) as i:
                    for h in range(2):
                        b = 2 * i + h
                        hold(dve, "dve", out_ps.sem, out_ps.done(p, b - 2))
                        v.tensor_copy(stg[0:kk, h, :], acc[0:kk, bass.ds(b * BN, BN)]).then_inc(staged.sem, 1)
                    for h in range(2):
                        b = 2 * i + h
                        tiles = bass.ds(b * BT, BT)
                        dve.wait_ge(out_ps.sem, out_ps.done(p, b))
                        w = HID if p == "gin1" else C
                        got = ps[:, 4 + h, 0:BT * w].rearrange("p (t c) -> p t c", c=w)
                        if p == "gin1":
                            ins = v.tensor_tensor(tb_h[:, tiles, :], got,
                                                  b2r[:, :].unsqueeze(1).broadcast_to([P, BT, HID]), ALU.add)
                        elif p == "gin2":
                            ins = v.tensor_tensor(yn[:, tiles, :], got, b4r[:, :].unsqueeze(1).broadcast_to([P, BT, C]), ALU.add)
                        elif p == "apply":
                            ins = v.scalar_tensor_tensor(yn[:, tiles, :], got, 1.0 / HEADS,
                                                         abr[:, :].unsqueeze(1).broadcast_to([P, BT, C]), ALU.mult, ALU.add)
                        else:
                            scale, dst = {"gcn1": (dinv2, tb), "gcn2": (dinv, yn)}.get(p, (rcnt, yn))
                            ins = v.tensor_tensor(dst[:, tiles, :], got, over_features(scale[:, tiles], BT), ALU.mult)
                        ins.then_inc(out_done.sem, 1)
                dve.wait_ge(out_done.sem, out_done.done(p, BLOCKS - 1))

            def make_basis(tl, i, h):
                hold(dve, "dve", attr_in[h], (i + 1) * 16)
                hold(dve, "dve", bas_out[h], i * 16)
                a = attr[:, h, :, :]
                link_ = tl
                link_(v.tensor_scalar(a, a, float(KS - 1), float(KS - 1), ALU.mult, ALU.min))
                flat_hat = hat[:, :, :, :].rearrange("p t d k -> p (t d) k")
                link_(v.scalar_tensor_tensor(flat_hat, a.rearrange("p t d -> p (t d)").unsqueeze(2).broadcast_to([P, 3 * G, KS]),
                                             0.0, iota_f[:, 0:KS].unsqueeze(1).broadcast_to([P, 3 * G, KS]),
                                             ALU.max, ALU.subtract))
                link_(v.scalar_tensor_tensor(flat_hat, flat_hat, -1.0, flat_hat, ALU.mult, ALU.min))
                link_(v.tensor_scalar(flat_hat, flat_hat, 1.0, 0.0, ALU.add, ALU.max))
                v.tensor_copy(bas[:, h, :, 0:KS], hat[:, :, 0, :])
                v.tensor_tensor(bas[:, h, :, KS:].rearrange("p t (a b) -> p t a b", b=KS),
                                hat[:, :, 2, :].unsqueeze(3).broadcast_to([P, G, KS, KS]),
                                hat[:, :, 1, :].unsqueeze(2).broadcast_to([P, G, KS, KS]), ALU.mult).then_inc(bas_ready.sem, 1)

            def one_hots(p, k, h):
                hold(dve, "dve", sums_ready.sem, sums_ready.done(p, SUBS * (k - 2) + SUBS - 1))
                v.tensor_tensor(oh[:, h, :, :], iota_f[:, 0:WIN].unsqueeze(1).broadcast_to([P, G, WIN]),
                                loc[:, bass.ds(k * G, G)].unsqueeze(2).broadcast_to([P, G, WIN]),
                                ALU.is_equal).then_inc(onehot_ready.sem, 1)

            def add_windows(p, k, s, firsts):
                m, g = acc_rows(p), SUBS * k + s
                hold(dve, "dve", sums_ready.sem, sums_ready.done(p, g))
                for q in range(SUB):
                    window = acc[0:m, bass.ds(firsts[s * SUB + q], WIN)]
                    dve.wait_ge(added.sem, added.done(p, SUB * g + q - 1))
                    v.tensor_tensor(window, window, ps[0:m, 6 + s % 2, q * WIN:(q + 1) * WIN], ALU.add)\
                     .then_inc(added.sem, 1)

            def weight_rows(p, k, h, s, close=False):
                g, t0 = SUBS * k + s, s * SUB
                if p == "apply":
                    hold(dve, "dve", sums_ready.sem, sums_ready.done(p, g - 2))
                    wts = tilech[:, 0:HEADS, bass.ds(k * G + t0, SUB)].rearrange("p h t -> p t h")
                else:
                    if close:
                        hold(dve, "dve", mom_ps.sem, mom_ps.done(p, SUB * (g - 2) + SUB - 1))
                    else:
                        hold(dve, "dve", ut_ps.sem, ut_ps.done(p, g - 2))
                    wts = bs[:, h, t0:t0 + SUB, 0:KS]
                v.tensor_tensor(u0[:, s % 2, :, :].rearrange("p t (a c) -> p t a c", c=C),
                                rows(p, h)[:, t0:t0 + SUB, 0:C].unsqueeze(2).broadcast_to([P, SUB, 4, C]),
                                wts.unsqueeze(3).broadcast_to([P, SUB, 4, C]), ALU.mult).then_inc(u_ready.sem, 1)

            def messages(p, k, h, s, half, tl):
                u, t0 = 2 * (SUBS * k + s) + half, s * SUB + 2 * half
                z = ps[:, 2 + 2 * half:4 + 2 * half, :].rearrange("p t (k c) -> p t k c", c=C)
                dve.wait_ge(z_ready.sem, z_ready.done(p, u))
                v.tensor_tensor(zb[:, half, :, :, :], z,
                                bs[:, h, t0:t0 + 2, KS:].unsqueeze(3).broadcast_to([P, 2, K12, C]),
                                ALU.mult).then_inc(y_ready.sem, 1)
                dve.wait_ge(y_ready.sem, y_ready.done(p, u))
                v.tensor_reduce(msg[:, s % 2, 2 * half:2 * half + 2, :],
                                zb[:, half, :, :, :].rearrange("p t k c -> p t c k"),
                                axis=AX.X, op=ALU.add).then_inc(msg_ready.sem, 1)

            def edge_pass(p):
                with dve.Fori(0, TURNS) as i:
                    tl = TurnLink(i, 8) if p == "gin1" else None
                    for h in range(2):
                        k = 2 * i + h
                        dve.load(regs, base[0:1, bass.ds(k * G, G)])
                        firsts = [dve.snap(r, min_val=0, max_val=N) for r in regs]
                        if p in SPLINE:
                            hold(dve, "dve", gathered[p][h], (i + 1) * (16 * G))
                            hold(dve, "dve", basis_in[h], (i + 1) * 16 + 16 * TURNS * SPLINE.index(p))
                            weight_rows(p, k, h, 0)
                            weight_rows(p, k, h, 1)
                            one_hots(p, k, h)
                            for s in range(SUBS):
                                messages(p, k, h, s, 0, tl)
                                messages(p, k, h, s, 1, tl)
                                if s + 2 < SUBS:
                                    weight_rows(p, k, h, s + 2)
                                if s >= 1:
                                    add_windows(p, k, s - 1, firsts)
                            add_windows(p, k, SUBS - 1, firsts)
                        elif p == "apply":
                            one_hots(p, k, h)
                            hold(dve, "dve", rows_in[h], (i + 1) * 16)
                            weight_rows(p, k, h, 0)
                            weight_rows(p, k, h, 1)
                            for s in range(SUBS):
                                add_windows(p, k, s, firsts)
                                if s + 2 < SUBS:
                                    weight_rows(p, k, h, s + 2)
                        else:
                            one_hots(p, k, h)
                            if p == "gin1":
                                make_basis(tl, i, h)
                            for s in range(SUBS):
                                add_windows(p, k, s, firsts)
                if p == "gin1":
                    tl.close(TURNS)

            def moments(p):
                def close_one_hots(k, h):
                    v.tensor_tensor(oh_close[:, h, :, :], iota_f[:, 0:TW].unsqueeze(1).broadcast_to([P, G, TW]),
                                    loc[:, bass.ds(k * G, G)].unsqueeze(2).broadcast_to([P, G, TW]),
                                    ALU.is_equal).then_inc(close_made, 1)

                def rows_here(k, h, turn_):
                    hold(dve, "dve", gathered[p][h], (turn_ + 1) * (16 * G))
                    hold(dve, "dve", basis_in[h], (turn_ + 1) * 16 + 16 * TURNS * SPLINE.index(p))

                def one_hot_basis(k, h, t):
                    if t == 0:
                        hold(dve, "dve", close_made, k + (1 + halves * SPLINE.index(p)))
                    hold(dve, "dve", mom_ps.sem, mom_ps.done(p, G * k + t - SUB))
                    v.tensor_tensor(vb[:, t % SUB, :, :], bs[:, h, t, KS:].unsqueeze(2).broadcast_to([P, K12, TW]),
                                    oh_close[:, h, t, :].unsqueeze(1).broadcast_to([P, K12, TW]),
                                    ALU.mult).then_inc(v_ready.sem, 1)

                def add_moments(k, h, t, at_):
                    n = G * k + t
                    hold(dve, "dve", mom_ps.sem, mom_ps.done(p, n))
                    dve.wait_ge(mom_added.sem, mom_added.done(p, n - 1))
                    to = mom[:, h, :, bass.ds(at_, TW)]
                    got = ps[:, t % SUB, 0:K12 * TW].rearrange("p (k j) -> p k j", j=TW)
                    v.tensor_tensor(to, to, got, ALU.add).then_inc(mom_added.sem, 1)

                def add_aggregate(k, h):
                    first = dve.value_load(half_prev[0:1, bass.ds(k, 1)], min_val=0, max_val=N)
                    hold(dve, "dve", agg_ps.sem, agg_ps.done(p, k))
                    dve.wait_ge(agg_added.sem, agg_added.done(p, k - 1))
                    to = acc[0:C, bass.ds(first, GW)]
                    v.tensor_tensor(to, to, ps[0:C, 4 + h, 0:GW], ALU.add).then_inc(agg_added.sem, 1)

                def turn_(i, last):
                    for h in range(2):
                        k = 2 * i + h
                        more = not (last and h == 1)
                        if more:
                            close_one_hots(k + 1, 1 - h)
                        dve.load(regs, offs[0:1, bass.ds(k * G, G)])
                        places = [dve.snap(r, min_val=0, max_val=GW - 1) for r in regs]
                        hold(dve, "dve", mom_zero.sem, mom_zero.done(p, k + 1))
                        for t in range(G):
                            add_moments(k, h, t, places[t])
                            if t + SUB < G:
                                one_hot_basis(k, h, t + SUB)
                            elif more:
                                one_hot_basis(k + 1, 1 - h, t + SUB - G)
                            s = t // SUB
                            if t % SUB == SUB - 1 and s + 2 < SUBS:
                                weight_rows(p, k, h, s + 2, close=True)
                            elif t % SUB == SUB - 1 and more:
                                weight_rows(p, k + 1, 1 - h, s + 2 - SUBS, close=True)
                            if t == G - SUB - 2 and more:
                                rows_here(k + 1, 1 - h, i + h)
                            if t == G - 2:
                                add_aggregate(k, h)

                close_one_hots(0, 0)
                rows_here(0, 0, 0)
                weight_rows(p, 0, 0, 0, close=True)
                weight_rows(p, 0, 0, 1, close=True)
                for t in range(SUB):
                    one_hot_basis(0, 0, t)
                with dve.Fori(0, TURNS - 1) as i:
                    turn_(i, False)
                turn_(TURNS - 1, True)
                add_aggregate(2 * TURNS, 0)

            def half_sums(p):
                near = xc_flat[:, 0:ET].bitcast(I32)
                first_of = xc_flat[:, ET:ET + 2 * TURNS].bitcast(I32)
                by_half = (lambda a: a.rearrange("p (k t) -> p k t", t=G))
                dve.wait_ge(near_in, 32)
                v.tensor_tensor(by_half(xc_flat[:, 0:ET]), by_half(near),
                                first_of.unsqueeze(2).broadcast_to([P, 2 * TURNS, G]),
                                ALU.subtract).then_inc(near_made, 1)
                dve.wait_ge(near_made, 1)

                def add_half(k, h, first):
                    hold(dve, "dve", sums_ready.sem, sums_ready.done(p, SUBS * k + SUBS - 1))
                    dve.wait_ge(agg_added.sem, agg_added.done(p, k - 1))
                    to = acc[:, bass.ds(first, GW)]
                    v.tensor_tensor(to, to, ps[:, 4 + h, 0:GW], ALU.add).then_inc(agg_added.sem, 1)

                def near_one_hots(k, h):
                    hold(dve, "dve", sums_ready.sem, sums_ready.done(p, SUBS * (k - 2) + SUBS - 1))
                    v.tensor_tensor(oh_half[:, h, :, :], iota_f[:, :].unsqueeze(1).broadcast_to([P, G, GW]),
                                    xc_flat[:, bass.ds(k * G, G)].unsqueeze(2).broadcast_to([P, G, GW]),
                                    ALU.is_equal).then_inc(onehot_ready.sem, 1)

                def turn_(i, first=False, last=False):
                    dve.load(regs[0:2], half_prev[0:1, bass.ds(2 * i, 2)])
                    firsts = [dve.snap(r, min_val=0, max_val=N) for r in regs[0:2]]
                    for h in range(2):
                        k = 2 * i + h
                        if not (last and h == 1):
                            near_one_hots(k + 1, 1 - h)
                        if not (first and h == 0):
                            add_half(k - 1, 1 - h, firsts[h])

                near_one_hots(0, 0)
                turn_(0, first=True)
                with dve.Fori(1, TURNS - 1) as i:
                    turn_(i)
                turn_(TURNS - 1, last=True)
                add_half(2 * TURNS - 1, 1, dve.value_load(half_prev[0:1, 2 * TURNS:2 * TURNS + 1], min_val=0, max_val=N))

            def chunk_turns(name, n):
                with dve.Fori(0, n // 2) as i:
                    for h in range(2):
                        c = 2 * i + h
                        hold(dve, "dve", cturn_ps.sem, cturn_ps.done(name, c - 2))
                        if name == "rows":
                            src = nodes[:, bass.ds(c * ET, ET)].rearrange("p (q r) -> p r q", r=RCH)
                        else:
                            src = big[:, bass.ds(c * ET, ET)].rearrange("p (r q) -> p r q", r=RCH)
                        v.tensor_copy(cst[h].rearrange("p (r q) -> p r q", r=RCH), src).then_inc(cstaged.sem, 1)
                dve.wait_ge(cturned.sem, cturned.done(name, n - 1))

            def scan_rows(chans, op0, op1, penalty, neutral, backward):
                way = (lambda a: a[:, ::-1]) if backward else (lambda a: a)
                end = 0 if backward else ET - 1
                for c, (dst, src) in enumerate(chans):
                    link(v.tensor_tensor_scan(t1, way(penalty), way(src), neutral, op0, op1))
                    link(v.tensor_copy(car[:, c:c + 1], t1[:, ET - 1:ET]))
                link(v.tensor_reduce(pen8[:, 0:1], penalty, axis=AX.X, op=ALU.min))
                link(v.tensor_copy(pen8[:, 1:SCAL], pen8[:, 0:1].broadcast_to([P, SCAL - 1])))
                ask_pe(v.tensor_copy(car[:, :], car[:, :]))
                link(v.tensor_copy(carr[:, :], ps[0:SCAL, 5, 0:P]))
                ask_pe(v.tensor_copy(pen8[:, :], pen8[:, :]))
                link(v.tensor_copy(penr[:, :], ps[0:SCAL, 5, P:2 * P]))
                edge, dst = (P, carry[:, 0:P]) if backward else (0, carry[:, 1:P + 1])
                link(v.memset(carry[:, edge:edge + 1], neutral))
                ask_pe(v.tensor_tensor_scan(way(dst), way(penr[:, :]), way(carr[:, :]), neutral, op0, op1))
                link(v.tensor_copy(init[:, :], ps[:, 6, 0:SCAL]))
                for c, (dst, src) in enumerate(chans):
                    link(v.tensor_tensor_scan(way(dst), way(penalty), way(src), init[:, c:c + 1], op0, op1))

            def penalties():
                dve.wait_ge(seg_in, 16 * 4)
                for pen in (pen_f, pen_b, pen_self):
                    link(v.tensor_tensor(pen, t1.bitcast(I32), pen.bitcast(I32), ALU.not_equal))
                    link(v.tensor_scalar(pen, pen, -BIG, None, ALU.mult))

            def attention():
                seg = nodes[:, 0:HEADS * ET]
                segch = [nodes[:, c * ET:(c + 1) * ET] for c in range(HEADS)]
                d = [rowch[:, c, :] for c in range(HEADS)]
                s = [rowch[:, HEADS + c, :] for c in range(HEADS)]
                dall, sall = big[:, 0:HEADS * ET], big[:, HEADS * ET:2 * HEADS * ET]
                for c in range(HEADS):
                    link(v.scalar_tensor_tensor(s[c], s[c], fcb[:, :], pen_self, ALU.add, ALU.add))
                up = [(segch[c], d[c]) for c in range(HEADS)] + [(s[c], s[c]) for c in range(HEADS)]
                down = [(o, o) for o, _ in up]
                scan_rows(up, ALU.add, ALU.max, pen_f, -BIG, False)
                scan_rows(down, ALU.add, ALU.max, pen_b, -BIG, True)
                link(v.tensor_tensor(dall, dall, sall, ALU.add))
                link(v.scalar_tensor_tensor(dall, dall, 0.2, dall, ALU.mult, ALU.max))
                link(v.tensor_tensor(seg, seg, sall, ALU.add))
                link(v.scalar_tensor_tensor(seg, seg, 0.2, seg, ALU.mult, ALU.max))
                ask_act(v.tensor_tensor(dall, dall, seg, ALU.subtract))
                link(v.tensor_scalar(cont, pen_f, 0.0, None, ALU.is_equal))
                up = [(segch[c], d[c]) for c in range(HEADS)]
                scan_rows(up, ALU.mult, ALU.add, cont, 0.0, False)
                scan_rows([(o, o) for o, _ in up], ALU.add, ALU.max, pen_b, -BIG, True)
                link(v.reciprocal(seg, seg))
                link(v.tensor_tensor(dall, dall, seg, ALU.mult))

            def table():
                link(v.tensor_copy(stat[:, 0:1], epsc[:, :]))
                dve.sem_inc(table_ready, 1)

            for h in range(2):
                link(v.memset(rows("gin1", h)[:, :, C:], 1.0))
            dve.sem_inc(ones_set, 1)
            link(v.memset(acc[:, :], 0.0))
            dve.wait_ge(consts, 6)
            dve.wait_ge(xload, 16 * 4)
            link(v.memset(epsc[:, :], EPS))
            link(v.memset(car[:, :], 0.0))
            link(v.tensor_copy(iota_f[:, :], iota_i[:, :]))
            link(v.tensor_tensor(loc[:, :], target.bitcast(I32), first_target.bitcast(I32), ALU.subtract))
            turn("x")
            link(v.memset(zero[:, :], 0.0))
            link(v.memset(half_prev[:, 0:1], 0))
            link(v.tensor_copy(half_prev[:, 1:], base.rearrange("p (k t) -> p k t", t=G)[:, :, 0]))
            by_half = (lambda a: a.rearrange("p (k t) -> p k t", t=G))
            first = by_half(first_target.bitcast(I32))[:, :, 0:1].broadcast_to([P, ET // G, G])
            own = by_half(base[0:1, :])[:, :, 0:1].broadcast_to([1, ET // G, G])
            link(v.tensor_tensor(by_half(offs[:, :]), by_half(base[:, :]), own, ALU.subtract))
            link(v.tensor_tensor(by_half(target), by_half(target.bitcast(I32)), first, ALU.subtract))
            link(v.tensor_scalar(target, target, float(TW - GW), None, ALU.add))
            link(v.tensor_tensor(target, target, loc[:, :], ALU.max))
            ask_pe(v.tensor_reduce(far[:, :], target, axis=AX.X, op=ALU.max))
            link(v.tensor_reduce(far[0:1, :], ps[0:1, 7, 0:P], axis=AX.X, op=ALU.max))
            link(v.tensor_scalar(far_i[:, :], far[0:1, :], TW - 0.5, None, ALU.is_gt))
            dve.sem_inc(far_known, 1)

            edge_pass("gin1")
            dve.wait_ge(added.sem, added.done("gin1", ET - 1))
            dve.sem_inc(counted, 1)
            dve.wait_ge(loads, 16 * len(LOADS))
            node_phase("gin1")
            link(v.tensor_scalar(tb_h, tb_h, 0.0, None, ALU.max))
            table()
            for which in range(2):
                part = vtmp[:, which * HEADS:(which + 1) * HEADS, :]
                link(v.tensor_tensor(part, whf[:, :, :], fcr[:, 1 - which, :].unsqueeze(1).broadcast_to([P, HEADS, C]), ALU.mult))
            link(v.tensor_reduce(v8r[:, :], vtmp[:, :, :], axis=AX.X, op=ALU.add))
            link(v.memset(v8[:, :], 0.0))
            for q in range(QT):
                link(v.tensor_copy(v8[q * C:(q + 1) * C, q * SCAL:(q + 1) * SCAL], v8r[q * C:(q + 1) * C, :]))
            dve.wait_ge(fm_done.sem, fm_done.done("gin1", BLOCKS - 1))
            dve.wait_ge(cnt_in, 16)
            ask_pe(v.tensor_copy(cnt_rows[:, :], cnt_rows[:, :]))
            link(v.tensor_copy(cnt[:, :], ps[:, 7, 0:NT]))
            link(v.tensor_scalar(rcnt[:, :], cnt[:, :], 1.0, None, ALU.max))
            link(v.reciprocal(rcnt[:, :], rcnt[:, :]))
            link(v.tensor_scalar(dinv2[:, :], cnt[:, :], 1.0, 1.0, ALU.add, ALU.max))
            edge_pass("gin2")
            node_phase("gin2")
            link(v.tensor_tensor(yn, yn, xn[:, :, :], ALU.add))
            layer_norm()
            ask_act(v.tensor_copy(dinv2[:, :], dinv2[:, :]))
            link(v.reciprocal(dinv[:, :], stat[:, :]))
            link(v.tensor_tensor(dinv2[:, :], dinv[:, :], dinv[:, :], ALU.mult))

            link(v.tensor_scalar(tb, xn[:, :, :], 0.0, None, ALU.max))
            link(v.tensor_tensor(tb, tb, over_features(dinv[:, :]), ALU.mult))
            table()
            turn("gin2")
            edge_pass("gcn1")
            node_phase("gcn1")
            table()
            turn("gcn1")
            edge_pass("gcn2")
            node_phase("gcn2")
            link(v.tensor_tensor(yn, yn, xn[:, :, :], ALU.add))
            layer_norm()

            link(v.tensor_copy(xc[:, :, :], xn[:, :, :]))
            for l, p in enumerate(SPLINE):
                table()
                link(v.memset(acc[0:C, :], 0.0))
                turn(p)
                two_ways(dve, "dve", p, moments, edge_pass)
                node_phase(p)
                link(v.tensor_tensor(yn, yn, rn, ALU.add))
                if l < 2:
                    link(v.scalar_tensor_tensor(yn, yn, 0.01, yn, ALU.mult, ALU.max))
                link(v.tensor_tensor(yn, yn, xc[:, :, :], ALU.add))
                batch_norm(l)
            link(v.tensor_tensor(yn, xn[:, :, :], xc[:, :, :], ALU.add))
            layer_norm()

            link(v.tensor_copy(tb_att[:, :, 0:C], xn[:, :, :]))
            turn("collect")
            table()
            penalties()
            for h in range(2):
                dve.wait_ge(rows_out[h], 16 * TURNS)
            dve.wait_ge(scal_copied.sem, scal_copied.done("collect", halves - 1))
            chunk_turns("rows", SCAL)
            attention()
            chunk_turns("tiles", HEADS)
            table()
            link(v.memset(acc[:, :], 0.0))
            two_ways(dve, "dve", "apply", half_sums, edge_pass)
            node_phase("apply")
            link(v.tensor_tensor(yn, yn, xn[:, :, :], ALU.add))
            layer_norm()
            table()


def kernel(x, src, dst, edge_attr_3, L0_gnn_W1, L0_gnn_b1, L0_gnn_W2, L0_gnn_b2, L0_gnn_W3, L0_gnn_b3, L0_gnn_W4,
           L0_gnn_b4, L2_gnn_W1, L2_gnn_R1, L2_gnn_b1, L2_gnn_g1, L2_gnn_be1, L2_gnn_W2, L2_gnn_R2, L2_gnn_b2,
           L2_gnn_g2, L2_gnn_be2, L2_gnn_W3, L2_gnn_R3, L2_gnn_b3, L2_gnn_g3, L2_gnn_be3, L3_gnn_w, L3_gnn_fc_w,
           L3_gnn_fc_b, L3_gnn_bias):
    import numpy as np
    import concourse.bacc as bacc
    from concourse.bass_utils import run_bass_kernel_spmd

    x, src, dst, attr = (np.asarray(a) for a in (x, src, dst, edge_attr_3))
    x_pad = np.concatenate([x, np.zeros((NP - N, C), x.dtype)])
    pad = np.full(P * ET - E, N, src.dtype)
    src_pad, dst_pad = np.concatenate([src, pad]), np.concatenate([dst, pad])
    attr_pad = np.concatenate([attr, np.zeros((P * ET - E, 3), attr.dtype)])
    outside = np.full(1, -1, dst.dtype)
    arrays = {
        "x": x_pad,
        "src_tile": src_pad.reshape(ET, P).T,
        "dst_tile": dst_pad.reshape(ET, P).T,
        "dst_base": dst_pad.reshape(ET, P)[:, 0].reshape(1, ET),
        "half_base": dst_pad.reshape(ET // G, G * P)[:, 0].reshape(1, ET // G),
        "src_row": src_pad.reshape(P, ET),
        "dst_ext": np.concatenate([outside, dst_pad, outside]),
        "attr_tile": attr_pad.reshape(ET, P, 3).transpose(1, 0, 2).reshape(P, ET * 3),
        "gW1": L0_gnn_W1, "gb1": L0_gnn_b1, "gW2": L0_gnn_W2, "gb2": L0_gnn_b2,
        "gW3": L0_gnn_W3, "gb3": L0_gnn_b3, "gW4": L0_gnn_W4, "gb4": L0_gnn_b4,
        "sW1": L2_gnn_W1, "sW2": L2_gnn_W2, "sW3": L2_gnn_W3, "sR1": L2_gnn_R1, "sR2": L2_gnn_R2, "sR3": L2_gnn_R3,
        "sb1": L2_gnn_b1, "sb2": L2_gnn_b2, "sb3": L2_gnn_b3, "sg1": L2_gnn_g1, "sg2": L2_gnn_g2, "sg3": L2_gnn_g3,
        "sbe1": L2_gnn_be1, "sbe2": L2_gnn_be2, "sbe3": L2_gnn_be3,
        "aw": L3_gnn_w, "fc_w": L3_gnn_fc_w, "fc_b": L3_gnn_fc_b, "abias": L3_gnn_bias,
    }
    arrays = {f"in_{k}": np.ascontiguousarray(v) for k, v in arrays.items()}
    nc = bacc.Bacc("TRN2", target_bir_lowering=False, num_devices=1)
    ap = {k[3:]: nc.dram_tensor(k, a.shape, mybir.dt.from_np(a.dtype), kind="ExternalInput").ap() for k, a in arrays.items()}
    out = nc.dram_tensor("out", (N, C), F32, kind="ExternalOutput").ap()

    def three(name):
        return [ap.pop(f"{name}{l}") for l in (1, 2, 3)]

    spline = {"sW": three("sW"), "sR": three("sR"), "sb_": three("sb"), "sg": three("sg"), "sbe": three("sbe")}
    build(nc, **ap, **spline, out=out)
    r = run_bass_kernel_spmd(nc, [arrays], core_ids=[0])
    return r.results[0]["out"]
```
